# Optimizing a Trainium2 kernel written in Bass

```python
import numpy as np
import jax
import jax.numpy as jnp

def _softmax(x, axis=-1):
    return jax.nn.softmax(x, axis=axis)

def _gelu(x):
    return jax.nn.gelu(x, approximate=True)

def _silu(x):
    return jax.nn.silu(x)

def _sigmoid(x):
    return jax.nn.sigmoid(x)

def _layernorm(x, axis=-1, eps=1e-05):
    m = jnp.mean(x, axis=axis, keepdims=True)
    v = jnp.var(x, axis=axis, keepdims=True)
    return (x - m) / jnp.sqrt(v + eps)

def _scatter_add(tgt, idx, src, axis=0):
    return tgt.at[idx].add(src)

def _segment_sum(src, seg, n):
    return jax.ops.segment_sum(src, seg, n)
kernel_name = 'mk_adj_resnorm_d1_adj_r2_7bb461'

def setup_inputs(seed: int=0):
    np.random.seed(seed)
    _w = jnp.asarray

    def _rec_inputs():
        import jax
        import jax.numpy as jnp
        _gk = jax.random.key(seed)
        x = 7.22e-05 + 1 * jax.random.normal(jax.random.fold_in(_gk, 1), (16, 512, 512), jnp.float32)
        _w = (1.0 + jnp.arange(512, dtype=jnp.float32)) ** (-0.5)
        _w = _w / _w.mean()
        _pij = jnp.clip(0.0078125 * _w[:, None] * _w[None, :], 0.0, 1.0)
        _a = jax.random.uniform(jax.random.fold_in(_gk, 2), (512, 512)) < _pij
        _a = jnp.logical_or(_a, jnp.eye(512, dtype=bool))
        _af = _a.astype(jnp.float32)
        adj = _af
        return (x, adj)
    x, adj = _rec_inputs()

    def _L0_gnn_setup():
        import jax, jax.numpy as jnp
        import numpy as np
        EPS = 1e-08

        def _row_stochastic_causal(A, causal_mask):
            A = A * causal_mask
            deg = jnp.maximum(A.sum(axis=-1, keepdims=True), EPS)
            return A / deg
        key = jax.random.key(seed)
        k = jax.random.split(key, 5)
        B, N, D = (4, 1024, 512)
        s = 1.0 / np.sqrt(D)
        h = jax.random.normal(k[0], (B, N, D), dtype=jnp.float32)
        W_lang = jax.random.normal(k[1], (D, D), dtype=jnp.float32) * s
        W_grav = jax.random.normal(k[2], (D, D), dtype=jnp.float32) * s
        W_V = jax.random.normal(k[3], (D, D), dtype=jnp.float32) * s
        W_O = jax.random.normal(k[4], (D, D), dtype=jnp.float32) * s
        causal_mask = jnp.tril(jnp.ones((N, N), dtype=jnp.float32))
        gate_logit = jnp.zeros((), jnp.float32)
        log_sigma = jnp.zeros((), jnp.float32)
        return {'h': h, 'causal_mask': causal_mask, 'W_lang': W_lang, 'W_grav': W_grav, 'W_V': W_V, 'W_O': W_O, 'gate_logit': gate_logit, 'log_sigma': log_sigma}
    _L0_gnn_all = _L0_gnn_setup()
    _L0_gnn_in = {k: v for k, v in _L0_gnn_all.items() if k in ('W_lang', 'W_grav', 'W_V', 'W_O', 'gate_logit', 'log_sigma')}
    del _L0_gnn_all
    return {'x': x, 'adj': adj, 'L0_gnn_W_lang': _L0_gnn_in['W_lang'], 'L0_gnn_W_grav': _L0_gnn_in['W_grav'], 'L0_gnn_W_V': _L0_gnn_in['W_V'], 'L0_gnn_W_O': _L0_gnn_in['W_O'], 'L0_gnn_gate_logit': _L0_gnn_in['gate_logit'], 'L0_gnn_log_sigma': _L0_gnn_in['log_sigma']}

def reference(x, adj, L0_gnn_W_lang, L0_gnn_W_grav, L0_gnn_W_V, L0_gnn_W_O, L0_gnn_gate_logit, L0_gnn_log_sigma):
    import jax
    import jax.numpy as jnp

    def _L0_gnn_ref(h, causal_mask, W_lang, W_grav, W_V, W_O, gate_logit, log_sigma):
        import jax, jax.numpy as jnp
        import numpy as np
        EPS = 1e-08

        def _row_stochastic_causal(A, causal_mask):
            A = A * causal_mask
            deg = jnp.maximum(A.sum(axis=-1, keepdims=True), EPS)
            return A / deg
        z_l = jnp.einsum('bnd,ed->bne', h, W_lang)
        z_g = jnp.einsum('bnd,ed->bne', h, W_grav)
        v = jnp.einsum('bnd,ed->bne', h, W_V)
        N = h.shape[-2]
        not_eye = 1.0 - jnp.eye(N, dtype=h.dtype)
        zn = z_l / jnp.maximum(jnp.linalg.norm(z_l, axis=-1, keepdims=True), EPS)
        A_l = jnp.maximum(jnp.einsum('bnd,bmd->bnm', zn, zn), 0.0) * not_eye
        sq = jnp.sum(z_g * z_g, axis=-1, keepdims=True)
        d2 = jnp.maximum(sq + jnp.swapaxes(sq, -1, -2) - 2.0 * jnp.einsum('bnd,bmd->bnm', z_g, z_g), 0.0)
        sigma = jnp.exp(log_sigma)
        A_g = jnp.exp(-d2 / (2.0 * sigma * sigma)) * not_eye
        K_l = _row_stochastic_causal(A_l, causal_mask)
        K_g = _row_stochastic_causal(A_g, causal_mask)
        w_l = jax.nn.sigmoid(gate_logit)
        K = w_l * K_l + (1.0 - w_l) * K_g
        out = jnp.einsum('bnm,bmd->bnd', K, v)
        return jnp.einsum('bnd,ed->bne', out, W_O)
    x = _layernorm(x + _L0_gnn_ref(x, adj, L0_gnn_W_lang, L0_gnn_W_grav, L0_gnn_W_V, L0_gnn_W_O, L0_gnn_gate_logit, L0_gnn_log_sigma), axis=-1)
    return x

_drawn_inputs = setup_inputs


def setup_inputs(seed=0):
    import zlib

    import numpy as np

    out = dict(_drawn_inputs(seed))
    spreads = {}
    factors = {}
    for name, (base, spread) in spreads.items():
        noise = np.random.default_rng([zlib.crc32(name.encode()), seed]).standard_normal(out[name].shape)
        drawn = base * np.exp(spread * noise) if base else spread * noise
        out[name] = jnp.asarray(drawn.astype(out[name].dtype))
    for name, factor in factors.items():
        out[name] = (out[name] * factor).astype(out[name].dtype)
    return out
```

```python
from contextlib import ExitStack

import concourse.bass as bass
from concourse import mybir

ALU = mybir.AluOpType
ACT = mybir.ActivationFunctionType
F32 = mybir.dt.float32
F32R = mybir.dt.float32r

P = 128
EPS_DEG = 1e-8
EPS_NORM = 1e-8
EPS_LN = 1e-5
RING = 3

G_BLOCKS = [(0, 1, 2), (1, 2, 3), (2, 3), (0, 3)]
OFF_BLOCKS = [(i, j) for i in range(4) for j in G_BLOCKS[i] if j != i]

PROLOGUE = ([("xT0", k) for k in range(4)] + [("wgT", k) for k in range(4)]
            + [("wlT", 0), ("wlT", 1), ("zg", 0), ("wlT", 2), ("zg", 1), ("wlT", 3), ("zg", 2), ("woT", 0),
               ("zg", 3), ("woT", 1), ("zl", 0), ("woT", 2), ("zl", 1), ("woT", 3), ("zl", 2)]
            + [("wvo", k) for k in range(4)] + [("zl", 3)]
            + [("u", k) for k in range(4)] + [("xT1", k) for k in range(4)])


class Order:

    def __init__(self, has_next, has_after):
        names = []
        if has_next:
            names += [("zg", i) for i in range(4)] + [("zl", i) for i in range(4)] + [("u", i) for i in range(3)]
        names += [("kT", 0)] + [("u", 3)] * has_next + [("kT", 1), ("out", 0)]
        names += [("xT", 0)] * has_after + [("kT", 2), ("out", 1)] + [("xT", 1)] * has_after
        names += [("kT", 3), ("out", 2)] + [("xT", 2)] * has_after + [("out", 3)] + [("xT", 3)] * has_after
        self.at = {name: n for n, name in enumerate(names)}
        split = [name for name in names if name[0] != "out"]
        self.hi = {name: n for n, name in enumerate(split)}
        self.tiles, self.splits = len(names), len(split)


def graph_attention(nc, x, adj, w_lang, w_grav, w_v, w_o, gate_logit, log_sigma, out):
    B, N, D = x.shape
    T = N // P
    assert N == D == 4 * P and B >= 4 and B % 2 == 0
    n_pro = len(PROLOGUE)
    inner = Order(True, True)
    assert n_pro % RING == 0 and inner.tiles % RING == 0

    x_rows = x.rearrange("b (t p) d -> b p t d", p=P)
    out_rows = out.rearrange("b (t p) d -> b t p d", p=P)

    def natural(w):
        return w.rearrange("(t p) d -> p t d", p=P)

    with ExitStack() as ctx:
        def sb(name, shape, dt=F32):
            return ctx.enter_context(nc.sbuf_tensor(name, shape, dt))

        def sem(name):
            return ctx.enter_context(nc.semaphore(name))

        def hi_lo(name):
            return sb(name + "_hi", [P, T, D], F32R), sb(name + "_lo", [P, T, D], F32R)

        wgT, wlT, wvo = hi_lo("wgT"), hi_lo("wlT"), hi_lo("wvo")
        xT, zg, zl, kT = hi_lo("xT"), hi_lo("zg"), hi_lo("zl"), hi_lo("kT")
        u = [hi_lo("u_even"), hi_lo("u_odd")]
        xt = sb("xt", [P, T, D])
        y = sb("y", [P, T, D])
        ag = sb("ag", [P, T, N])
        al = sb("al", [P, T, N])
        mask = sb("mask", [P, T, N])
        mask_r = sb("mask_r", [P, T, N])
        off = sb("off", [P, len(OFF_BLOCKS), P])
        hsq_row = sb("hsq_row", [P, N])
        r_row = sb("r_row", [P, N])
        ident = sb("ident", [P, P])
        diag_out = sb("diag_out", [P, T, P])
        hsq = sb("hsq", [P, T])
        nsq = sb("nsq", [P, T])
        nsq_max = sb("nsq_max", [P, T])
        r = sb("r", [P, T])
        sum_g = sb("sum_g", [P, T])
        sum_l = sb("sum_l", [P, T])
        deg = sb("deg", [P, 6, T])
        scale_g = sb("scale_g", [P, T])
        scale_l = sb("scale_l", [P, T])
        bn = sb("bn", [P, T, 6])
        mv = sb("mv", [P, T, 2])
        var_eps = sb("var_eps", [P, T])
        rstd = sb("rstd", [P, T])
        neg_half = sb("neg_half", [P, T])
        scal = sb("scal", [P, 12])
        gate_in, sig_in = scal[:, 0:1], scal[:, 1:2]
        gate_exp, sigma, gate_1p = scal[:, 2:3], scal[:, 3:4], scal[:, 4:5]
        w_l, w_g, sigma2, inv_sigma2 = scal[:, 5:6], scal[:, 6:7], scal[:, 7:8], scal[:, 8:9]
        wg_nat, wl_nat, wo_nat, wv_nat, wv, woT = al, ag, mask_r, y, u[1], kT

        g_bank = [ctx.enter_context(nc.psum_tensor(f"g_bank{i}", [P, N], F32)) for i in range(T)]
        ring = [ctx.enter_context(nc.psum_tensor(f"ring{i}", [P, N], F32)) for i in range(RING)]
        row_bank = ctx.enter_context(nc.psum_tensor("row_bank", [P, N], F32))

        xt_loaded, y_loaded, stored = sem("xt_loaded"), sem("y_loaded"), sem("stored")
        wg_loaded, wl_loaded, wo_loaded = sem("wg_loaded"), sem("wl_loaded"), sem("wo_loaded")
        wv_loaded, adj_loaded, scalars_loaded = sem("wv_loaded"), sem("adj_loaded"), sem("scalars_loaded")
        ident_cleared, ident_ready, mask_ready = sem("ident_cleared"), sem("ident_ready"), sem("mask_ready")
        neg_half_ready, scalar_exps, scalar_step = sem("neg_half_ready"), sem("scalar_exps"), sem("scalar_step")
        wv_hi, wv_split = sem("wv_hi"), sem("wv_split")
        stream_ready, hi_written, evacuated = sem("stream_ready"), sem("hi_written"), sem("evacuated")
        gg_rows, gg_diag, gg_off, gg_full = sem("gg_rows"), sem("gg_diag"), sem("gg_off"), sem("gg_full")
        gl_rows, gl_diag, gl_off, gl_full = sem("gl_rows"), sem("gl_diag"), sem("gl_off"), sem("gl_full")
        hsq_in_psum, hsq_row_ready = sem("hsq_in_psum"), sem("hsq_row_ready")
        r_clamped, r_ready, r_in_psum = sem("r_clamped"), sem("r_ready"), sem("r_in_psum")
        r_row_ready, mask_r_ready = sem("r_row_ready"), sem("mask_r_ready")
        exp_arg, exp_done, ag_masked, ag_scaled = sem("exp_arg"), sem("exp_done"), sem("ag_masked"), sem("ag_scaled")
        al_masked, k_ready = sem("al_masked"), sem("k_ready")
        deg_step = sem("deg_step")
        DEG_G, DEG_ALL = 3, 7
        bn_written, moments, var_ready, rstd_ready, y_done = (
            sem("bn_written"), sem("moments"), sem("var_ready"), sem("rstd_ready"), sem("y_done"))

        block = ctx.enter_context(nc.Block())

        def all_batches(engine, batch):
            with engine.Fori(0, (B - 2) // 2) as pair:
                for parity in range(2):
                    b = pair * 2 + parity
                    batch(b, True, True, parity, b * inner.tiles + n_pro, b * inner.splits + n_pro)
            n0, h0 = (B - 2) * inner.tiles + n_pro, (B - 2) * inner.splits + n_pro
            batch(B - 2, True, False, 0, n0, h0)
            last = Order(True, False)
            batch(B - 1, False, False, 1, n0 + last.tiles, h0 + last.splits)

        def first_bank(has_next):
            return 0 if has_next else Order(True, False).tiles % RING

        @block.sync
        def _(sp):
            for half in range(2):
                rows = slice(half * T // 2, (half + 1) * T // 2)
                sp.dma_start(xt[:, rows, :], x_rows[0][:, rows, :]).then_inc(xt_loaded, 16)
            sp.dma_start(wl_nat[:, :, :], natural(w_lang)).then_inc(wl_loaded, 16)
            sp.dma_start(wv_nat[:, :, :], natural(w_v)).then_inc(wv_loaded, 16)
            sp.dma_start(mask[:, :, :], natural(adj)).then_inc(adj_loaded, 16)
            sp.wait_ge(stream_ready, 4)
            sp.dma_start(xt[:, :, :], x_rows[1]).then_inc(xt_loaded, 16)
            sp.wait_ge(wv_split, 1)
            sp.dma_start(y[:, :, :], x_rows[0]).then_inc(y_loaded, 16)

            def batch(b, has_next, has_after, parity, n0, h0):
                if has_after:
                    sp.wait_ge(stream_ready, n0)
                    sp.dma_start(xt[:, :, :], x_rows[b + 2]).then_inc(xt_loaded, 16)
                for i in range(T):
                    sp.wait_ge(y_done, b * T + (i + 1))
                    sp.dma_start(out_rows[b][i], y[:, i, :]).then_inc(stored, 16)
                if has_next:
                    sp.wait_ge(stored, b * (16 * T) + 16 * T)
                    sp.dma_start(y[:, :, :], x_rows[b + 1]).then_inc(y_loaded, 16)

            all_batches(sp, batch)
            sp.wait_ge(stored, 16 * T * B)

        @block.tensor
        def _(pe):
            def claim_bank(n):
                if not isinstance(n, int) or n >= RING:
                    pe.wait_ge(evacuated, n - (RING - 1))

            def transposed(bank, blocks):
                for j, blk in enumerate(blocks):
                    last = nc.tensor.transpose(bank[:, j * P:(j + 1) * P], blk, ident[:, :])
                last.then_inc(stream_ready, 1)

            def product(psum, left, right):
                for k in range(T):
                    (lh, ll), (rh, rl) = left(k), right(k)
                    nc.tensor.matmul(psum, lh, rh, start=k == 0, stop=False)
                    nc.tensor.matmul(psum, lh, rl, start=False, stop=False)
                    last = nc.tensor.matmul(psum, ll, rh, start=False, stop=k == T - 1)
                return last

            def column_block(pair, i):
                return lambda k: tuple(t[:, k, i * P:(i + 1) * P] for t in pair)

            def whole_row(pair):
                return lambda k: tuple(t[:, k, :] for t in pair)

            def project(bank, kind, i, u_next):
                if kind == "zg":
                    last = product(bank[:, :], column_block(wgT, i), whole_row(xT))
                elif kind == "zl":
                    last = product(bank[:, :], column_block(wlT, i), whole_row(xT))
                else:
                    last = product(bank[:, :], column_block(xT, i), whole_row(wvo))
                last.then_inc(stream_ready, 1)

            def gram_row(z, i, rows_done):
                step = G_BLOCKS[i][1] - G_BLOCKS[i][0]
                cols = slice(G_BLOCKS[i][0], G_BLOCKS[i][-1] + 1, step)
                psum = g_bank[i][:, :].rearrange("p (c n) -> p c n", n=P)[:, cols, :]
                right = [t[:, :, :].rearrange("p k (c n) -> p k c n", n=P) for t in z]
                product(psum, column_block(z, i), lambda k: tuple(t[:, k, cols, :] for t in right))\
                    .then_inc(rows_done, 1)

            def mirror(full):
                for s, (i, j) in enumerate(OFF_BLOCKS):
                    last = nc.tensor.transpose(g_bank[j][:, i * P:(i + 1) * P], off[:, s, :], ident[:, :])
                last.then_inc(full, 1)

            def column_as_row(col, done):
                for t in range(T):
                    last = nc.tensor.transpose(row_bank[:, t * P:(t + 1) * P],
                                               col[:, t:t + 1].to_broadcast([P, P]), ident[:, :])
                last.then_inc(done, 1)

            pe.wait_ge(ident_ready, 1)
            place = {name: n for n, name in enumerate(PROLOGUE)}
            for n, (kind, i) in enumerate(PROLOGUE):
                bank = ring[n % RING]
                claim_bank(n)
                if kind in ("xT0", "xT1", "wgT", "wlT", "woT"):
                    if i == 0:
                        pe.wait_ge(*{"xT0": (xt_loaded, 32), "xT1": (xt_loaded, 48), "wgT": (wg_loaded, 16),
                                     "wlT": (wl_loaded, 16), "woT": (wo_loaded, 16)}[kind])
                    src = {"xT0": xt, "xT1": xt, "wgT": wg_nat, "wlT": wl_nat, "woT": wo_nat}[kind]
                    transposed(bank, [src[:, j, i * P:(i + 1) * P] for j in range(T)])
                elif kind == "wvo":
                    if i == 0:
                        pe.wait_ge(wv_split, 1)
                        pe.wait_ge(evacuated, place[("woT", T - 1)] + 1)
                    product(bank[:, :], column_block(wv, i), whole_row(woT)).then_inc(stream_ready, 1)
                else:
                    if i == 0:
                        pe.wait_ge(evacuated, place[({"zg": "wgT", "zl": "wlT", "u": "wvo"}[kind], T - 1)] + 1)
                    project(bank, kind, i, 0)

            def batch(b, has_next, has_after, parity, n0, h0):
                order = Order(has_next, has_after)
                first = first_bank(has_next)

                def begin(name):
                    claim_bank(n0 + order.at[name])
                    return ring[(first + order.at[name]) % RING]

                def attend(i):
                    bank = begin(("kT", i))
                    pe.wait_ge(k_ready, b * T + (i + 1))
                    transposed(bank, [al[:, i, j * P:(j + 1) * P] for j in range(T)])

                def aggregate(i):
                    bank = begin(("out", i))
                    pe.wait_ge(evacuated, n0 + (order.at[("kT", i)] + 1))
                    kT_i = [t[:, i, :].rearrange("p (k n) -> p k n", n=P) for t in kT]
                    product(bank[:, :], lambda k: tuple(t[:, k, :] for t in kT_i), whole_row(u[parity]))\
                        .then_inc(stream_ready, 1)

                def transpose_x(i):
                    bank = begin(("xT", i))
                    if i == 0:
                        pe.wait_ge(xt_loaded, b * 16 + 64)
                    transposed(bank, [xt[:, j, i * P:(i + 1) * P] for j in range(T)])

                for i in range(T):
                    gram_row(zg, i, gg_rows)
                if has_next:
                    pe.wait_ge(evacuated, n0)
                    project(begin(("zg", 0)), "zg", 0, None)
                pe.wait_ge(gg_off, b * T + T)
                mirror(gg_full)
                column_as_row(hsq, hsq_in_psum)
                if has_next:
                    for i in range(1, T):
                        project(begin(("zg", i)), "zg", i, None)
                for i in range(T):
                    pe.wait_ge(exp_arg, b * T + (i + 1))
                    gram_row(zl, i, gl_rows)
                if has_next:
                    project(begin(("zl", 0)), "zl", 0, None)
                pe.wait_ge(gl_off, b * T + T)
                mirror(gl_full)
                pe.wait_ge(r_ready, b + 1)
                pe.wait_ge(hsq_row_ready, b + 1)
                column_as_row(r, r_in_psum)
                if has_next:
                    for i in range(1, T):
                        project(begin(("zl", i)), "zl", i, None)
                    for i in range(3):
                        project(begin(("u", i)), "u", i, None)
                attend(0)
                if has_next:
                    project(begin(("u", 3)), "u", 3, None)
                attend(1)
                for i in range(T):
                    aggregate(i)
                    if has_after:
                        transpose_x(i)
                    if i + 2 < T:
                        attend(i + 2)

            all_batches(pe, batch)

        @block.scalar
        def _(act):
            act.dma_start(wg_nat[:, :, :], natural(w_grav)).then_inc(wg_loaded, 16)
            act.dma_start(wo_nat[:, :, :], natural(w_o)).then_inc(wo_loaded, 16)
            act.dma_start(gate_in, gate_logit.to_broadcast([P, 1])).then_inc(scalars_loaded, 16)
            act.dma_start(sig_in, log_sigma.to_broadcast([P, 1])).then_inc(scalars_loaded, 16)

            def split_hi(bank, ready, pair, i):
                act.wait_ge(stream_ready, ready)
                nc.scalar.activation(pair[0][:, i, :], bank[:, :], ACT.Copy).then_inc(hi_written, 1)

            for n, (kind, i) in enumerate(PROLOGUE):
                pair = {"xT0": xT, "xT1": xT, "wgT": wgT, "wlT": wlT, "woT": woT, "wvo": wvo, "zg": zg,
                        "zl": zl, "u": u[0]}[kind]
                split_hi(ring[n % RING], n + 1, pair, i)
                if (kind, i) == ("wlT", 1):
                    act.wait_ge(wv_loaded, 16)
                    nc.scalar.activation(wv[0][:, :, :], wv_nat[:, :, :], ACT.Copy).then_inc(wv_hi, 1)
                if (kind, i) == ("zg", 1):
                    act.wait_ge(scalars_loaded, 32)
                    nc.scalar.activation(gate_exp, gate_in, ACT.Exp, scale=-1.0).then_inc(scalar_exps, 1)
                    nc.scalar.activation(sigma, sig_in, ACT.Exp).then_inc(scalar_exps, 1)

            act.wait_ge(scalar_step, 5)

            def batch(b, has_next, has_after, parity, n0, h0):
                order = Order(has_next, has_after)
                first = first_bank(has_next)

                def hi(name, pair):
                    split_hi(ring[(first + order.at[name]) % RING], n0 + (order.at[name] + 1), pair, name[1])

                def copy_off(i, diag_read, done):
                    act.wait_ge(diag_read, b * T + (i + 1))
                    mine = [s for s, (a, _) in enumerate(OFF_BLOCKS) if a == i]
                    j0 = OFF_BLOCKS[mine[0]][1]
                    nc.scalar.activation(off[:, mine[0]:mine[-1] + 1, :],
                                         g_bank[i][:, j0 * P:(j0 + len(mine)) * P]
                                         .rearrange("p (c n) -> p c n", n=P), ACT.Copy).then_inc(done, 1)

                def exp_row(i):
                    act.wait_ge(exp_arg, b * T + (i + 1))
                    nc.scalar.activation(ag[:, i, :], ag[:, i, :], ACT.Exp, scale=inv_sigma2).then_inc(exp_done, 1)

                for i in range(T):
                    copy_off(i, gg_diag, gg_off)
                if has_next:
                    hi(("zg", 0), zg)
                act.wait_ge(hsq_in_psum, b + 1)
                nc.scalar.activation(hsq_row[:, :], row_bank[:, :], ACT.Copy).then_inc(hsq_row_ready, 1)
                exp_row(0)
                if has_next:
                    hi(("zg", 1), zg)
                exp_row(1)
                exp_row(2)
                if has_next:
                    hi(("zg", 2), zg)
                exp_row(3)
                if has_next:
                    hi(("zg", 3), zg)
                for i in range(T):
                    copy_off(i, gl_diag, gl_off)
                if has_next:
                    hi(("zl", 0), zl)
                act.wait_ge(r_in_psum, b + 1)
                nc.scalar.activation(r_row[:, :], row_bank[:, :], ACT.Copy).then_inc(r_row_ready, 1)
                if has_next:
                    hi(("zl", 1), zl)
                act.wait_ge(deg_step, b * DEG_ALL + DEG_G)
                for i in range(T):
                    nc.scalar.activation(ag[:, i, :], ag[:, i, :], ACT.Copy, scale=scale_g[:, i:i + 1])\
                        .then_inc(ag_scaled, 1)
                if has_next:
                    for i in range(2, T):
                        hi(("zl", i), zl)
                    for i in range(3):
                        hi(("u", i), u[1 - parity])
                hi(("kT", 0), kT)
                if has_next:
                    hi(("u", 3), u[1 - parity])
                hi(("kT", 1), kT)
                for i in range(T):
                    if has_after:
                        hi(("xT", i), xT)
                    if i + 2 < T:
                        hi(("kT", i + 2), kT)

            all_batches(act, batch)

        @block.vector
        def _(dve):
            def split_lo(bank, hi_count, pair, i):
                dve.wait_ge(hi_written, hi_count)
                nc.vector.tensor_tensor(pair[1][:, i, :], bank[:, :], pair[0][:, i, :].bitcast(F32),
                                        ALU.subtract).then_inc(evacuated, 1)

            for n, (kind, i) in enumerate(PROLOGUE):
                pair = {"xT0": xT, "xT1": xT, "wgT": wgT, "wlT": wlT, "woT": woT, "wvo": wvo, "zg": zg,
                        "zl": zl, "u": u[0]}[kind]
                split_lo(ring[n % RING], n + 1, pair, i)
                if (kind, i) == ("wlT", 1):
                    dve.wait_ge(wv_hi, 1)
                    nc.vector.tensor_tensor(wv[1][:, :, :], wv_nat[:, :, :], wv[0][:, :, :].bitcast(F32),
                                            ALU.subtract).then_inc(wv_split, 1)
                if (kind, i) == ("zg", 1):
                    dve.wait_ge(scalar_exps, 2)
                    nc.vector.tensor_scalar_add(gate_1p, gate_exp, 1.0).then_inc(scalar_step, 1)
                    nc.vector.tensor_tensor(sigma2, sigma, sigma, ALU.mult).then_inc(scalar_step, 1)
                    dve.wait_ge(scalar_step, 2)
                    nc.vector.reciprocal(w_l, gate_1p).then_inc(scalar_step, 1)
                    nc.vector.reciprocal(inv_sigma2, sigma2).then_inc(scalar_step, 1)
                    dve.wait_ge(scalar_step, 4)
                    nc.vector.tensor_scalar(w_g, w_l, -1.0, 1.0, ALU.mult, ALU.add).then_inc(scalar_step, 1)
            dve.wait_ge(scalar_step, 5)
            dve.wait_ge(ident_ready, 1)
            dve.wait_ge(mask_ready, 1)

            def batch(b, has_next, has_after, parity, n0, h0):
                order = Order(has_next, has_after)
                first = first_bank(has_next)

                def bank(name):
                    return ring[(first + order.at[name]) % RING]

                def lo(name, pair):
                    split_lo(bank(name), h0 + (order.hi[name] + 1), pair, name[1])

                def diagonal(i, rows_done, factor, col, done):
                    dve.wait_ge(rows_done, b * T + (i + 1))
                    nc.vector.scalar_tensor_tensor(
                        out=diag_out[:, i, :], in0=g_bank[i][:, i * P:(i + 1) * P], scalar=factor,
                        in1=ident[:, :], op0=ALU.mult, op1=ALU.mult, accum_out=col[:, i:i + 1]).then_inc(done, 1)

                def exponent(i):
                    nc.vector.scalar_tensor_tensor(
                        out=ag[:, i, :], in0=g_bank[i][:, :], scalar=hsq[:, i:i + 1], in1=hsq_row[:, :],
                        op0=ALU.subtract, op1=ALU.subtract).then_inc(exp_arg, 1)

                def mask_ag(i):
                    dve.wait_ge(exp_done, b * T + (i + 1))
                    nc.vector.scalar_tensor_tensor(
                        out=ag[:, i, :], in0=ag[:, i, :], scalar=1.0, in1=mask[:, i, :],
                        op0=ALU.min, op1=ALU.mult, accum_out=sum_g[:, i:i + 1]).then_inc(ag_masked, 1)

                def mask_al(i):
                    nc.vector.scalar_tensor_tensor(
                        out=al[:, i, :], in0=g_bank[i][:, :], scalar=0.0, in1=mask_r[:, i, :],
                        op0=ALU.max, op1=ALU.mult, accum_out=sum_l[:, i:i + 1]).then_inc(al_masked, 1)

                def combine(i):
                    dve.wait_ge(ag_scaled, b * T + (i + 1))
                    nc.vector.scalar_tensor_tensor(
                        out=al[:, i, :], in0=al[:, i, :], scalar=scale_l[:, i:i + 1], in1=ag[:, i, :],
                        op0=ALU.mult, op1=ALU.add).then_inc(k_ready, 1)

                def residual(i):
                    dve.wait_ge(stream_ready, n0 + (order.at[("out", i)] + 1))
                    nc.vector.tensor_tensor(y[:, i, :], bank(("out", i))[:, :], y[:, i, :], ALU.add)\
                        .then_inc(evacuated, 1)
                    dve.wait_ge(evacuated, n0 + (order.at[("out", i)] + 1))
                    nc.vector.bn_stats(bn[:, i, :], y[:, i, :]).then_inc(bn_written, 1)

                def statistics(i):
                    dve.wait_ge(mask_ready, 1)
                    dve.wait_ge(bn_written, b * T + (i + 1))
                    nc.vector.bn_aggr(mv[:, i, :], bn[:, i, :]).then_inc(moments, 1)
                    dve.wait_ge(moments, b * T + (i + 1))
                    nc.vector.tensor_scalar_add(var_eps[:, i:i + 1], mv[:, i, 1:2], EPS_LN).then_inc(var_ready, 1)

                def normalise(i):
                    dve.wait_ge(rstd_ready, b * T + (i + 1))
                    nc.vector.tensor_scalar(y[:, i, :], y[:, i, :], mv[:, i, 0:1], rstd[:, i:i + 1],
                                            ALU.subtract, ALU.mult).then_inc(y_done, 1)

                for i in range(T):
                    diagonal(i, gg_rows, 0.5, hsq, gg_diag)
                if has_next:
                    lo(("zg", 0), zg)
                dve.wait_ge(gg_full, b + 1)
                dve.wait_ge(hsq_row_ready, b + 1)
                exponent(0)
                exponent(1)
                exponent(2)
                exponent(3)
                if has_next:
                    lo(("zg", 1), zg)
                mask_ag(0)
                mask_ag(1)
                if has_next:
                    lo(("zg", 2), zg)
                mask_ag(2)
                if has_next:
                    lo(("zg", 3), zg)
                mask_ag(3)
                dve.wait_ge(ag_masked, b * T + T)
                nc.vector.tensor_scalar_max(deg[:, 0, :], sum_g[:, :], EPS_DEG).then_inc(deg_step, 1)
                dve.wait_ge(deg_step, b * DEG_ALL + 1)
                nc.vector.reciprocal(deg[:, 1, :], deg[:, 0, :]).then_inc(deg_step, 1)
                dve.wait_ge(deg_step, b * DEG_ALL + 2)
                nc.vector.tensor_scalar_mul(scale_g[:, :], deg[:, 1, :], w_g).then_inc(deg_step, 1)
                for i in range(T):
                    diagonal(i, gl_rows, 1.0, nsq, gl_diag)
                dve.wait_ge(gl_diag, b * T + T)
                nc.vector.tensor_scalar_max(nsq_max[:, :], nsq[:, :], EPS_NORM * EPS_NORM).then_inc(r_clamped, 1)
                if has_next:
                    for i in range(T):
                        lo(("zl", i), zl)
                dve.wait_ge(gl_full, b + 1)
                dve.wait_ge(mask_r_ready, b + 1)
                mask_al(0)
                mask_al(1)
                if has_next:
                    lo(("u", 0), u[1 - parity])
                mask_al(2)
                mask_al(3)
                dve.wait_ge(al_masked, b * T + T)
                nc.vector.tensor_tensor(deg[:, 2, :], sum_l[:, :], r[:, :], ALU.mult).then_inc(deg_step, 1)
                dve.wait_ge(deg_step, b * DEG_ALL + 4)
                nc.vector.tensor_scalar_max(deg[:, 3, :], deg[:, 2, :], EPS_DEG).then_inc(deg_step, 1)
                dve.wait_ge(deg_step, b * DEG_ALL + 5)
                nc.vector.reciprocal(deg[:, 4, :], deg[:, 3, :]).then_inc(deg_step, 1)
                dve.wait_ge(deg_step, b * DEG_ALL + 6)
                nc.vector.scalar_tensor_tensor(out=scale_l[:, :], in0=deg[:, 4, :], scalar=w_l, in1=r[:, :],
                                               op0=ALU.mult, op1=ALU.mult).then_inc(deg_step, 1)
                dve.wait_ge(deg_step, b * DEG_ALL + 7)
                combine(0)
                combine(1)
                if has_next:
                    lo(("u", 1), u[1 - parity])
                combine(2)
                combine(3)
                if has_next:
                    lo(("u", 2), u[1 - parity])
                lo(("kT", 0), kT)
                if has_next:
                    lo(("u", 3), u[1 - parity])
                lo(("kT", 1), kT)
                dve.wait_ge(y_loaded, b * 16 + 16)
                for i in range(T):
                    residual(i)
                    if has_after:
                        lo(("xT", i), xT)
                    statistics(i)
                    if i + 2 < T:
                        lo(("kT", i + 2), kT)
                    if i:
                        normalise(i - 1)
                normalise(T - 1)

            all_batches(dve, batch)

        @block.gpsimd
        def _(pool):
            nc.gpsimd.memset(ident[:, :], 0.0).then_inc(ident_cleared, 1)
            nc.gpsimd.memset(neg_half[:, :], -0.5).then_inc(neg_half_ready, 1)
            pool.wait_ge(ident_cleared, 1)
            nc.gpsimd.affine_select(out=ident[:, :], in_=ident[:, :], compare_op=ALU.not_equal, fill=1.0, base=0,
                                    pattern=[[-1, P]], channel_multiplier=1).then_inc(ident_ready, 1)
            pool.wait_ge(adj_loaded, 16)
            nc.gpsimd.affine_select(out=mask[:, :, :], in_=mask[:, :, :], compare_op=ALU.not_equal, fill=0.0,
                                    base=0, pattern=[[P, T], [-1, N]], channel_multiplier=1).then_inc(mask_ready, 1)
            pool.wait_ge(neg_half_ready, 1)
            pool.wait_ge(mask_ready, 1)

            def batch(b, has_next, has_after, parity, n0, h0):
                pool.wait_ge(r_clamped, b + 1)
                nc.gpsimd.tensor_tensor(r[:, :], nsq_max[:, :], neg_half[:, :], ALU.pow).then_inc(r_ready, 1)
                pool.wait_ge(r_row_ready, b + 1)
                nc.gpsimd.tensor_tensor(mask_r[:, :, :], mask[:, :, :],
                                        r_row[:, :].unsqueeze(1).to_broadcast([P, T, N]), ALU.mult)\
                    .then_inc(mask_r_ready, 1)
                for i in range(T):
                    pool.wait_ge(var_ready, b * T + (i + 1))
                    nc.gpsimd.tensor_tensor(rstd[:, i:i + 1], var_eps[:, i:i + 1], neg_half[:, 0:1], ALU.pow)\
                        .then_inc(rstd_ready, 1)

            all_batches(pool, batch)


_INS = ["x", "adj", "L0_gnn_W_lang", "L0_gnn_W_grav", "L0_gnn_W_V", "L0_gnn_W_O", "L0_gnn_gate_logit",
        "L0_gnn_log_sigma"]


def kernel(**inputs):
    import numpy as _np
    import concourse.bacc as _bacc
    from concourse import mybir as _mybir
    from concourse.bass_utils import run_bass_kernel_spmd as _run

    nc = _bacc.Bacc("TRN2", target_bir_lowering=False, num_devices=1)
    arrays, args = {}, []
    for name in _INS:
        a = _np.ascontiguousarray(inputs[name])
        if a.ndim < 2:
            a = a.reshape(1, 1)
        arrays[f"in_{name}_dram"] = a
        args.append(nc.dram_tensor(f"in_{name}_dram", a.shape, _mybir.dt.from_np(a.dtype), kind="ExternalInput").ap())
    shape = arrays["in_x_dram"].shape
    args.append(nc.dram_tensor("out_0_dram", shape, _mybir.dt.float32, kind="ExternalOutput").ap())
    graph_attention(nc, *args)
    r = _run(nc, [arrays], core_ids=[0])
    return r.results[0]["out_0_dram"]
```

```python
from contextlib import ExitStack

import concourse.bass as bass
from concourse import mybir

ALU = mybir.AluOpType
ACT = mybir.ActivationFunctionType
F32 = mybir.dt.float32
F32R = mybir.dt.float32r

P = 128
EPS_DEG = 1e-8
EPS_NORM = 1e-8
EPS_LN = 1e-5
RING = 4
Q = 32

G_BLOCKS = [(0, 1, 2), (1, 2, 3), (2, 3), (0, 3)]
OFF_BLOCKS = [(i, j) for i in range(4) for j in G_BLOCKS[i] if j != i]

PROLOGUE = ([("wgT", k) for k in range(4)]
            + [("wlT", 0), ("wlT", 1), ("zg", 0), ("wlT", 2), ("zg", 1), ("wlT", 3), ("zg", 2), ("woT", 0),
               ("zg", 3), ("woT", 1), ("zl", 0), ("woT", 2), ("zl", 1), ("woT", 3), ("zl", 2)]
            + [("wvo", k) for k in range(4)] + [("zl", 3)] + [("u", k) for k in range(4)])

BATCH = ([("zg", 1, 0), ("hsq", 0, 0), ("zg", 1, 1), ("zg", 1, 2), ("zg", 1, 3), ("zl", 1, 0), ("r", 0, 0),
          ("zl", 1, 1), ("zl", 1, 2), ("zl", 1, 3), ("u", 1, 0), ("u", 1, 1), ("u", 1, 2), ("kT", 0, 0),
          ("u", 1, 3), ("kT", 0, 1), ("out", 0, 0), ("kT", 0, 2), ("out", 0, 1), ("kT", 0, 3), ("out", 0, 2),
          ("out", 0, 3)])
LAST = (BATCH[:10]
        + [("kT", 0, 0), ("kT", 0, 1), ("out", 0, 0), ("hsq", 1, 0), ("kT", 0, 2), ("out", 0, 1), ("kT", 0, 3),
           ("out", 0, 2), ("out", 0, 3), ("r", 1, 0)]
        + [("u", 1, i) for i in range(4)]
        + [("kT", 1, 0), ("kT", 1, 1), ("out", 1, 0), ("kT", 1, 2), ("out", 1, 1), ("kT", 1, 3), ("out", 1, 2),
           ("out", 1, 3)])
SPLIT = ("zg", "zl", "u", "kT")


def splits(tiles):
    return [t for t in tiles if t[0] in SPLIT]


class Stream:

    def __init__(self, names, tiles, split, first):
        self.place = {t: n for n, t in enumerate(names)}
        self.place_split = {t: n for n, t in enumerate(splits(names))}
        self.tiles, self.split, self.first = tiles, split, first

    def number(self, name):
        return self.tiles + self.place[name]

    def upto(self, name):
        return self.tiles + (self.place[name] + 1)

    def split_upto(self, name):
        return self.split + (self.place_split[name] + 1)

    def bank(self, name):
        return (self.first + self.place[name]) % RING


def graph_attention(nc, x, adj, w_lang, w_grav, w_v, w_o, gate_logit, log_sigma, out):
    B, N, D = x.shape
    T = N // P
    QN = P // Q
    assert N == D == 4 * P and B >= 4 and B % 2 == 0
    n_pro = len(PROLOGUE)
    assert n_pro % RING == 0 and 2 * len(BATCH) % RING == 0

    x_rows = x.rearrange("b (t p) d -> b p t d", p=P)
    out_rows = out.rearrange("b (t p) d -> b t p d", p=P)
    x_blocks = x.rearrange("b (c j) (k a i) -> b a j k c i", j=Q, k=T, i=Q)

    def natural(w):
        return w.rearrange("(t p) d -> p t d", p=P)

    with ExitStack() as ctx:
        def sb(name, shape, dt=F32):
            return ctx.enter_context(nc.sbuf_tensor(name, shape, dt))

        def sem(name):
            return ctx.enter_context(nc.semaphore(name))

        def hi_lo(name):
            return sb(name + "_hi", [P, T, D], F32R), sb(name + "_lo", [P, T, D], F32R)

        wgT, wlT, wvo = hi_lo("wgT"), hi_lo("wlT"), hi_lo("wvo")
        xT, zg, zl, kT = hi_lo("xT"), hi_lo("zg"), hi_lo("zl"), hi_lo("kT")
        u = [hi_lo("u_even"), hi_lo("u_odd")]
        xb = sb("xb", [P, T, N])
        xT_whole = sb("xT_whole", [P, 2, N])
        y = sb("y", [P, T, D])
        ag = sb("ag", [P, T, N])
        al = sb("al", [P, T, N])
        mask = sb("mask", [P, T, N])
        mask_r = sb("mask_r", [P, T, N])
        off = sb("off", [P, len(OFF_BLOCKS), P])
        row = sb("row", [P, N])
        ident = sb("ident", [P, P])
        diag_out = sb("diag_out", [P, T, P], mybir.dt.bfloat16)
        hsq = sb("hsq", [P, T])
        nsq = sb("nsq", [P, T])
        wait_carrier = sb("wait_carrier", [P, 2, 2])
        hsq_wide = sb("hsq_wide", [P, P // T, T])
        r_wide = sb("r_wide", [P, P // T, T])
        nsq_max = sb("nsq_max", [P, T])
        r = sb("r", [P, T])
        sum_g = sb("sum_g", [P, T])
        sum_l = sb("sum_l", [P, T])
        deg = sb("deg", [P, 5, T])
        scale_g = sb("scale_g", [P, T])
        scale_l = sb("scale_l", [P, T])
        bn = sb("bn", [P, T, 6])
        mv = sb("mv", [P, T, 2])
        var_eps = sb("var_eps", [P, T])
        rstd = sb("rstd", [P, T])
        neg_half = sb("neg_half", [P, T])
        scal = sb("scal", [P, 12])
        gate_in, sig_in = scal[:, 0:1], scal[:, 1:2]
        gate_exp, sigma, gate_1p = scal[:, 2:3], scal[:, 3:4], scal[:, 4:5]
        w_l, w_g, sigma2, inv_sigma2 = scal[:, 5:6], scal[:, 6:7], scal[:, 7:8], scal[:, 8:9]
        wg_nat, wl_nat, wo_nat, wv_nat, wv, woT = al, ag, mask_r, y, u[1], kT

        g_bank = [ctx.enter_context(nc.psum_tensor(f"g_bank{i}", [P, N], F32)) for i in range(T)]
        ring = [ctx.enter_context(nc.psum_tensor(f"ring{i}", [P, N], F32)) for i in range(RING)]

        xb_loaded, y_loaded, stored = sem("xb_loaded"), sem("y_loaded"), sem("stored")
        wg_loaded = [sem(f"wg_loaded{k}") for k in range(T)]
        wl_loaded, wo_loaded, wv_loaded = sem("wl_loaded"), sem("wo_loaded"), sem("wv_loaded")
        adj_loaded, scalars_loaded = sem("adj_loaded"), sem("scalars_loaded")
        ident_cleared, ident_ready, mask_ready = sem("ident_cleared"), sem("ident_ready"), sem("mask_ready")
        neg_half_ready, scalar_exps, scalar_step = sem("neg_half_ready"), sem("scalar_exps"), sem("scalar_step")
        wv_hi, wv_split = sem("wv_hi"), sem("wv_split")
        xT_transposed, xT_hi, xT_split = sem("xT_transposed"), sem("xT_hi"), sem("xT_split")
        stream_ready, hi_written, evacuated = sem("stream_ready"), sem("hi_written"), sem("evacuated")
        gg_rows, gg_diag, gg_off, gg_full = sem("gg_rows"), sem("gg_diag"), sem("gg_off"), sem("gg_full")
        gl_rows, gl_diag, gl_off, gl_full = sem("gl_rows"), sem("gl_diag"), sem("gl_off"), sem("gl_full")
        r_clamped, r_ready, mask_r_ready = sem("r_clamped"), sem("r_ready"), sem("mask_r_ready")
        hsq_widened, r_widened = sem("hsq_widened"), sem("r_widened")
        exp_arg, exp_done, ag_masked, ag_scaled = sem("exp_arg"), sem("exp_done"), sem("ag_masked"), sem("ag_scaled")
        al_masked, k_ready = sem("al_masked"), sem("k_ready")
        deg_step = sem("deg_step")
        DEG_G, DEG_ALL = 3, 7
        bn_written, moments, var_ready, rstd_ready, y_done = (
            sem("bn_written"), sem("moments"), sem("var_ready"), sem("rstd_ready"), sem("y_done"))

        block = ctx.enter_context(nc.Block())

        def all_batches(engine, batch, last_two):
            per, per_split = len(BATCH), len(splits(BATCH))
            with engine.Fori(0, (B - 2) // 2) as pair:
                for parity in range(2):
                    b = pair * 2 + parity
                    batch(b, parity, Stream(BATCH, b * per + n_pro, b * per_split + n_pro, parity * per % RING))
            b = B - 2
            last_two(b, Stream(LAST, b * per + n_pro, b * per_split + n_pro, 0))

        @block.sync
        def _(sp):
            def load_blocks(b):
                for a in range(QN):
                    sp.dma_start(xb[a * Q:(a + 1) * Q, :, :].rearrange("j k (c i) -> j k c i", i=Q),
                                 x_blocks[b][a]).then_inc(xb_loaded, 16)

            def store_rows(b):
                for i in range(T):
                    sp.wait_ge(y_done, b * T + (i + 1))
                    sp.dma_start(out_rows[b][i], y[:, i, :]).then_inc(stored, 16)

            def load_residual(b):
                sp.wait_ge(stored, b * (16 * T))
                sp.dma_start(y[:, :, :], x_rows[b]).then_inc(y_loaded, 16)

            load_blocks(0)
            sp.dma_start(wl_nat[:, :, :], natural(w_lang)).then_inc(wl_loaded, 16)
            sp.dma_start(wv_nat[:, :, :], natural(w_v)).then_inc(wv_loaded, 16)
            sp.dma_start(mask[:, :, :], natural(adj)).then_inc(adj_loaded, 16)
            sp.wait_ge(xT_transposed, T)
            load_blocks(1)
            sp.wait_ge(wv_split, 1)
            sp.dma_start(y[:, :, :], x_rows[0]).then_inc(y_loaded, 16)

            def batch(b, parity, stream):
                sp.wait_ge(xT_transposed, b * T + 2 * T)
                load_blocks(b + 2)
                store_rows(b)
                load_residual(b + 1)

            def last_two(b, stream):
                store_rows(b)
                load_residual(b + 1)
                store_rows(b + 1)

            all_batches(sp, batch, last_two)
            sp.wait_ge(stored, 16 * T * B)

        @block.tensor
        def _(pe):
            def claim_bank(n):
                if not isinstance(n, int) or n >= RING:
                    pe.wait_ge(evacuated, n - (RING - 1))

            def transposed(bank, blocks):
                for j, blk in enumerate(blocks):
                    last = nc.tensor.transpose(bank[:, j * P:(j + 1) * P], blk, ident[:, :])
                last.then_inc(stream_ready, 1)

            def product(psum, left, right):
                for k in range(T):
                    (lh, ll), (rh, rl) = left(k), right(k)
                    nc.tensor.matmul(psum, lh, rh, start=k == 0, stop=False)
                    nc.tensor.matmul(psum, lh, rl, start=False, stop=False)
                    last = nc.tensor.matmul(psum, ll, rh, start=False, stop=k == T - 1)
                return last

            def column_block(pair, i):
                return lambda k: tuple(t[:, k, i * P:(i + 1) * P] for t in pair)

            def whole_row(pair):
                return lambda k: tuple(t[:, k, :] for t in pair)

            def project(bank, kind, i):
                if kind == "zg":
                    last = product(bank[:, :], column_block(wgT, i), whole_row(xT))
                elif kind == "zl":
                    last = product(bank[:, :], column_block(wlT, i), whole_row(xT))
                else:
                    last = product(bank[:, :], column_block(xT, i), whole_row(wvo))
                last.then_inc(stream_ready, 1)

            def gram_row(z, i, rows_done):
                step = G_BLOCKS[i][1] - G_BLOCKS[i][0]
                cols = slice(G_BLOCKS[i][0], G_BLOCKS[i][-1] + 1, step)
                psum = g_bank[i][:, :].rearrange("p (c n) -> p c n", n=P)[:, cols, :]
                right = [t[:, :, :].rearrange("p k (c n) -> p k c n", n=P) for t in z]
                product(psum, column_block(z, i), lambda k: tuple(t[:, k, cols, :] for t in right))\
                    .then_inc(rows_done, 1)

            def mirror(full):
                for s, (i, j) in enumerate(OFF_BLOCKS):
                    last = nc.tensor.transpose(g_bank[j][:, i * P:(i + 1) * P], off[:, s, :], ident[:, :])
                last.then_inc(full, 1)

            pe.wait_ge(ident_ready, 1)
            place = {name: n for n, name in enumerate(PROLOGUE)}
            for n, (kind, i) in enumerate(PROLOGUE):
                bank = ring[n % RING]
                claim_bank(n)
                if kind in ("wgT", "wlT", "woT"):
                    if kind == "wgT":
                        pe.wait_ge(wg_loaded[i], 16)
                    elif i == 0:
                        pe.wait_ge(wl_loaded if kind == "wlT" else wo_loaded, 16)
                    src = {"wgT": wg_nat, "wlT": wl_nat, "woT": wo_nat}[kind]
                    transposed(bank, [src[:, j, i * P:(i + 1) * P] for j in range(T)])
                elif kind == "wvo":
                    if i == 0:
                        pe.wait_ge(wv_split, 1)
                        pe.wait_ge(evacuated, place[("woT", T - 1)] + 1)
                    product(bank[:, :], column_block(wv, i), whole_row(woT)).then_inc(stream_ready, 1)
                else:
                    if i == 0:
                        pe.wait_ge(evacuated, place[({"zg": "wgT", "zl": "wlT", "u": "wvo"}[kind], T - 1)] + 1)
                        pe.wait_ge(xT_split, T)
                    project(bank, kind, i)

            class Steps:

                def __init__(self, b, stream):
                    self.b, self.stream = b, stream

                def begin(self, name):
                    claim_bank(self.stream.number(name))
                    return ring[self.stream.bank(name)]

                def gram_g(self, db):
                    for i in range(T):
                        gram_row(zg, i, gg_rows)

                def gram_l(self, db):
                    for i in range(T):
                        pe.wait_ge(exp_arg, (self.b + db) * T + (i + 1))
                        gram_row(zl, i, gl_rows)

                def mirror_g(self, db):
                    pe.wait_ge(gg_off, (self.b + db) * T + T)
                    mirror(gg_full)
                    pe.wait_ge(hsq_widened, (self.b + db) + 1)
                    self.column_as_rows("hsq", db, hsq_wide)

                def mirror_l(self, db):
                    pe.wait_ge(gl_off, (self.b + db) * T + T)
                    mirror(gl_full)
                    pe.wait_ge(r_widened, (self.b + db) + 1)
                    self.column_as_rows("r", db, r_wide)

                def column_as_rows(self, kind, db, wide):
                    bank = self.begin((kind, db, 0))
                    nc.tensor.transpose(bank[:, 0:P], wide[:, :, :].rearrange("p s t -> p (s t)"), ident[:, :])\
                        .then_inc(stream_ready, 1)

                def project(self, kind, i):
                    bank = self.begin((kind, 1, i))
                    if (kind, i) == ("zg", 0):
                        pe.wait_ge(xT_split, self.b * T + 2 * T)
                    project(bank, kind, i)

                def transpose_k(self, db, i):
                    bank = self.begin(("kT", db, i))
                    pe.wait_ge(k_ready, (self.b + db) * T + (i + 1))
                    transposed(bank, [al[:, i, j * P:(j + 1) * P] for j in range(T)])

                def aggregate(self, db, i, parity):
                    bank = self.begin(("out", db, i))
                    pe.wait_ge(evacuated, self.stream.upto(("kT", db, i)))
                    kT_i = [t[:, i, :].rearrange("p (k n) -> p k n", n=P) for t in kT]
                    product(bank[:, :], lambda k: tuple(t[:, k, :] for t in kT_i), whole_row(u[parity]))\
                        .then_inc(stream_ready, 1)

            def batch(b, parity, stream):
                s = Steps(b, stream)
                s.gram_g(0)
                s.project("zg", 0)
                s.mirror_g(0)
                for i in range(1, T):
                    s.project("zg", i)
                s.gram_l(0)
                s.project("zl", 0)
                s.mirror_l(0)
                for i in range(1, T):
                    s.project("zl", i)
                for i in range(3):
                    s.project("u", i)
                s.transpose_k(0, 0)
                s.project("u", 3)
                s.transpose_k(0, 1)
                for i in range(T):
                    s.aggregate(0, i, parity)
                    if i + 2 < T:
                        s.transpose_k(0, i + 2)

            def last_two(b, stream):
                s = Steps(b, stream)
                s.gram_g(0)
                s.project("zg", 0)
                s.mirror_g(0)
                for i in range(1, T):
                    s.project("zg", i)
                s.gram_l(0)
                s.project("zl", 0)
                s.mirror_l(0)
                for i in range(1, T):
                    s.project("zl", i)
                pe.wait_ge(evacuated, stream.upto(("zg", 1, T - 1)))
                pe.wait_ge(al_masked, b * T + T)
                s.gram_g(1)
                s.transpose_k(0, 0)
                s.transpose_k(0, 1)
                s.aggregate(0, 0, 0)
                s.mirror_g(1)
                s.transpose_k(0, 2)
                s.aggregate(0, 1, 0)
                s.transpose_k(0, 3)
                s.aggregate(0, 2, 0)
                s.gram_l(1)
                s.aggregate(0, 3, 0)
                s.mirror_l(1)
                for i in range(T):
                    s.project("u", i)
                s.transpose_k(1, 0)
                s.transpose_k(1, 1)
                for i in range(T):
                    s.aggregate(1, i, 1)
                    if i + 2 < T:
                        s.transpose_k(1, i + 2)

            all_batches(pe, batch, last_two)

        @block.scalar
        def _(act):
            for k in range(T):
                act.dma_start(wg_nat[:, :, k * P:(k + 1) * P], natural(w_grav)[:, :, k * P:(k + 1) * P])\
                    .then_inc(wg_loaded[k], 16)
            act.dma_start(wo_nat[:, :, :], natural(w_o)).then_inc(wo_loaded, 16)
            act.dma_start(gate_in, gate_logit.to_broadcast([P, 1])).then_inc(scalars_loaded, 16)
            act.dma_start(sig_in, log_sigma.to_broadcast([P, 1])).then_inc(scalars_loaded, 16)

            def split_hi(bank, ready, pair, i):
                act.wait_ge(stream_ready, ready)
                nc.scalar.activation(pair[0][:, i, :], bank[:, :], ACT.Copy).then_inc(hi_written, 1)

            def x_hi(b, k):
                act.wait_ge(xT_transposed, b * T + (k + 1))
                nc.scalar.activation(xT[0][:, k, :], xT_whole[:, k % 2, :], ACT.Copy).then_inc(xT_hi, 1)

            for k in range(T):
                x_hi(0, k)
            for n, (kind, i) in enumerate(PROLOGUE):
                pair = {"wgT": wgT, "wlT": wlT, "woT": woT, "wvo": wvo, "zg": zg, "zl": zl, "u": u[0]}[kind]
                split_hi(ring[n % RING], n + 1, pair, i)
                if (kind, i) == ("wlT", 1):
                    act.wait_ge(wv_loaded, 16)
                    nc.scalar.activation(wv[0][:, :, :], wv_nat[:, :, :], ACT.Copy).then_inc(wv_hi, 1)
                if (kind, i) == ("zg", 1):
                    act.wait_ge(scalars_loaded, 32)
                    nc.scalar.activation(gate_exp, gate_in, ACT.Exp, scale=-1.0).then_inc(scalar_exps, 1)
                    nc.scalar.activation(sigma, sig_in, ACT.Exp).then_inc(scalar_exps, 1)
            for k in range(T):
                x_hi(1, k)
            act.wait_ge(scalar_step, 5)

            class Steps:

                def __init__(self, b, stream):
                    self.b, self.stream = b, stream

                def hi(self, kind, db, i, pair):
                    name = (kind, db, i)
                    split_hi(ring[self.stream.bank(name)], self.stream.upto(name), pair, i)

                def copy_off(self, db, diag_read, done):
                    for i in range(T):
                        mine = [s for s, (a, _) in enumerate(OFF_BLOCKS) if a == i]
                        j0 = OFF_BLOCKS[mine[0]][1]
                        act.wait_ge(diag_read, (self.b + db) * T + (i + 1))
                        nc.scalar.activation(off[:, mine[0]:mine[-1] + 1, :],
                                             g_bank[i][:, j0 * P:(j0 + len(mine)) * P]
                                             .rearrange("p (c n) -> p c n", n=P), ACT.Copy).then_inc(done, 1)

                def widen(self, db, ready, count, col, wide, done):
                    act.wait_ge(ready, count)
                    nc.scalar.activation(wide[:, :, :], col[:, :].unsqueeze(1).to_broadcast([P, P // T, T]),
                                         ACT.Copy).then_inc(done, 1)

                def widen_hsq(self, db):
                    self.widen(db, gg_diag, (self.b + db) * T + T, hsq, hsq_wide, hsq_widened)

                def widen_r(self, db):
                    self.widen(db, r_ready, (self.b + db) + 1, r, r_wide, r_widened)

                def exp(self, db, i):
                    act.wait_ge(exp_arg, (self.b + db) * T + (i + 1))
                    nc.scalar.activation(ag[:, i, :], ag[:, i, :], ACT.Exp, scale=inv_sigma2).then_inc(exp_done, 1)

                def scale_ag(self, db):
                    act.wait_ge(deg_step, (self.b + db) * DEG_ALL + DEG_G)
                    for i in range(T):
                        nc.scalar.activation(ag[:, i, :], ag[:, i, :], ACT.Copy, scale=scale_g[:, i:i + 1])\
                            .then_inc(ag_scaled, 1)

            def until_zl(s):
                s.copy_off(0, gg_diag, gg_off)
                s.widen_hsq(0)
                s.hi("zg", 1, 0, zg)
                s.exp(0, 0)
                s.hi("zg", 1, 1, zg)
                s.exp(0, 1)
                s.exp(0, 2)
                s.hi("zg", 1, 2, zg)
                s.exp(0, 3)
                s.hi("zg", 1, 3, zg)
                s.copy_off(0, gl_diag, gl_off)
                s.widen_r(0)
                s.hi("zl", 1, 0, zl)
                s.hi("zl", 1, 1, zl)
                s.scale_ag(0)
                s.hi("zl", 1, 2, zl)
                s.hi("zl", 1, 3, zl)

            def batch(b, parity, stream):
                s = Steps(b, stream)
                until_zl(s)
                for i in range(3):
                    s.hi("u", 1, i, u[1 - parity])
                s.hi("kT", 0, 0, kT)
                s.hi("u", 1, 3, u[1 - parity])
                s.hi("kT", 0, 1, kT)
                for k in range(T):
                    x_hi(b + 2, k)
                    if k + 2 < T:
                        s.hi("kT", 0, k + 2, kT)

            def last_two(b, stream):
                s = Steps(b, stream)
                until_zl(s)
                s.copy_off(1, gg_diag, gg_off)
                s.widen_hsq(1)
                s.hi("kT", 0, 0, kT)
                s.hi("kT", 0, 1, kT)
                s.hi("kT", 0, 2, kT)
                s.exp(1, 0)
                s.exp(1, 1)
                s.exp(1, 2)
                s.hi("kT", 0, 3, kT)
                s.exp(1, 3)
                s.copy_off(1, gl_diag, gl_off)
                s.widen_r(1)
                s.scale_ag(1)
                for i in range(T):
                    s.hi("u", 1, i, u[1])
                for i in range(T):
                    s.hi("kT", 1, i, kT)

            all_batches(act, batch, last_two)

        @block.vector
        def _(dve):
            def split_lo(bank, hi_count, pair, i):
                dve.wait_ge(hi_written, hi_count)
                nc.vector.tensor_tensor(pair[1][:, i, :], bank[:, :], pair[0][:, i, :].bitcast(F32),
                                        ALU.subtract).then_inc(evacuated, 1)

            def x_transpose(b, k):
                if k == 0:
                    dve.wait_ge(xb_loaded, b * (16 * QN) + 16 * QN)
                if k >= 2:
                    dve.wait_ge(xT_split, b * T + (k - 1))
                elif not isinstance(b, int) or b > 0:
                    dve.wait_ge(xT_split, (b - 1) * T + (k + 3))
                nc.vector.transpose(xT_whole[:, k % 2, :], xb[:, k, :]).then_inc(xT_transposed, 1)

            def x_lo(b, k):
                dve.wait_ge(xT_hi, b * T + (k + 1))
                nc.vector.tensor_tensor(xT[1][:, k, :], xT_whole[:, k % 2, :], xT[0][:, k, :].bitcast(F32),
                                        ALU.subtract).then_inc(xT_split, 1)

            def x_split(b):
                x_transpose(b, 0)
                for k in range(T):
                    if k + 1 < T:
                        x_transpose(b, k + 1)
                    x_lo(b, k)

            x_split(0)
            for n, (kind, i) in enumerate(PROLOGUE):
                pair = {"wgT": wgT, "wlT": wlT, "woT": woT, "wvo": wvo, "zg": zg, "zl": zl, "u": u[0]}[kind]
                split_lo(ring[n % RING], n + 1, pair, i)
                if (kind, i) == ("wlT", 1):
                    dve.wait_ge(wv_hi, 1)
                    nc.vector.tensor_tensor(wv[1][:, :, :], wv_nat[:, :, :], wv[0][:, :, :].bitcast(F32),
                                            ALU.subtract).then_inc(wv_split, 1)
                if (kind, i) == ("zg", 1):
                    dve.wait_ge(scalar_exps, 2)
                    nc.vector.tensor_scalar_add(gate_1p, gate_exp, 1.0).then_inc(scalar_step, 1)
                    nc.vector.tensor_tensor(sigma2, sigma, sigma, ALU.mult).then_inc(scalar_step, 1)
                    dve.wait_ge(scalar_step, 2)
                    nc.vector.reciprocal(w_l, gate_1p).then_inc(scalar_step, 1)
                    nc.vector.reciprocal(inv_sigma2, sigma2).then_inc(scalar_step, 1)
                    dve.wait_ge(scalar_step, 4)
                    nc.vector.tensor_scalar(w_g, w_l, -1.0, 1.0, ALU.mult, ALU.add).then_inc(scalar_step, 1)
            x_split(1)
            dve.wait_ge(scalar_step, 5)
            dve.wait_ge(ident_ready, 1)
            dve.wait_ge(mask_ready, 1)

            class Steps:

                def __init__(self, b, stream):
                    self.b, self.stream = b, stream

                def rows(self, db, i):
                    return (self.b + db) * T + (i + 1)

                def lo(self, kind, db, i, pair):
                    name = (kind, db, i)
                    split_lo(ring[self.stream.bank(name)], self.stream.split_upto(name), pair, i)

                def diagonals(self, db, rows_done, factor, col, done):
                    for i in range(T):
                        dve.wait_ge(rows_done, self.rows(db, i))
                        nc.vector.scalar_tensor_tensor(
                            out=diag_out[:, i, :], in0=g_bank[i][:, i * P:(i + 1) * P], scalar=factor,
                            in1=ident[:, :], op0=ALU.mult, op1=ALU.mult, accum_out=col[:, i:i + 1])\
                            .then_inc(done, 1)

                def repeat_row(self, kind, db):
                    bank = ring[self.stream.bank((kind, db, 0))]
                    dve.wait_ge(stream_ready, self.stream.upto((kind, db, 0)))
                    nc.vector.memset(wait_carrier[:, ("hsq", "r").index(kind)], 0.0)
                    for t in range(T):
                        last = nc.vector.stream_shuffle(row[:, t * P:(t + 1) * P], bank[:, 0:P], [t] * Q)
                    last.then_inc(evacuated, 1)

                def exponent(self, db, i):
                    nc.vector.scalar_tensor_tensor(
                        out=ag[:, i, :], in0=g_bank[i][:, :], scalar=hsq[:, i:i + 1], in1=row[:, :],
                        op0=ALU.subtract, op1=ALU.subtract).then_inc(exp_arg, 1)

                def exponents(self, db):
                    self.repeat_row("hsq", db)
                    dve.wait_ge(gg_full, (self.b + db) + 1)
                    dve.wait_ge(evacuated, self.stream.upto(("hsq", db, 0)))
                    for i in range(T):
                        self.exponent(db, i)

                def mask_ag(self, db, i):
                    dve.wait_ge(exp_done, self.rows(db, i))
                    nc.vector.scalar_tensor_tensor(
                        out=ag[:, i, :], in0=ag[:, i, :], scalar=1.0, in1=mask[:, i, :],
                        op0=ALU.min, op1=ALU.mult, accum_out=sum_g[:, i:i + 1]).then_inc(ag_masked, 1)

                def scale_of_ag(self, db):
                    dve.wait_ge(ag_masked, self.rows(db, T - 1))
                    step = (self.b + db) * DEG_ALL
                    nc.vector.tensor_scalar_max(deg[:, 0, :], sum_g[:, :], EPS_DEG).then_inc(deg_step, 1)
                    dve.wait_ge(deg_step, step + 1)
                    nc.vector.reciprocal(deg[:, 1, :], deg[:, 0, :]).then_inc(deg_step, 1)
                    dve.wait_ge(deg_step, step + 2)
                    nc.vector.tensor_scalar_mul(scale_g[:, :], deg[:, 1, :], w_g).then_inc(deg_step, 1)

                def clamp_norms(self, db):
                    dve.wait_ge(gl_diag, self.rows(db, T - 1))
                    nc.vector.tensor_scalar_max(nsq_max[:, :], nsq[:, :], EPS_NORM * EPS_NORM)\
                        .then_inc(r_clamped, 1)

                def mask_al(self, db, i):
                    if i == 0:
                        dve.wait_ge(gl_full, (self.b + db) + 1)
                    dve.wait_ge(mask_r_ready, self.rows(db, i))
                    nc.vector.scalar_tensor_tensor(
                        out=al[:, i, :], in0=g_bank[i][:, :], scalar=0.0, in1=mask_r[:, i, :],
                        op0=ALU.max, op1=ALU.mult, accum_out=sum_l[:, i:i + 1]).then_inc(al_masked, 1)

                def scale_of_al(self, db):
                    dve.wait_ge(al_masked, self.rows(db, T - 1))
                    step = (self.b + db) * DEG_ALL
                    nc.vector.tensor_tensor(deg[:, 2, :], sum_l[:, :], r[:, :], ALU.mult).then_inc(deg_step, 1)
                    dve.wait_ge(deg_step, step + 4)
                    nc.vector.tensor_scalar_max(deg[:, 3, :], deg[:, 2, :], EPS_DEG).then_inc(deg_step, 1)
                    dve.wait_ge(deg_step, step + 5)
                    nc.vector.reciprocal(deg[:, 4, :], deg[:, 3, :]).then_inc(deg_step, 1)
                    dve.wait_ge(deg_step, step + 6)
                    nc.vector.scalar_tensor_tensor(out=scale_l[:, :], in0=deg[:, 4, :], scalar=w_l, in1=r[:, :],
                                                   op0=ALU.mult, op1=ALU.mult).then_inc(deg_step, 1)
                    dve.wait_ge(deg_step, step + 7)

                def combine(self, db, i):
                    dve.wait_ge(ag_scaled, self.rows(db, i))
                    nc.vector.scalar_tensor_tensor(
                        out=al[:, i, :], in0=al[:, i, :], scalar=scale_l[:, i:i + 1], in1=ag[:, i, :],
                        op0=ALU.mult, op1=ALU.add).then_inc(k_ready, 1)

                def residual(self, db, i):
                    name = ("out", db, i)
                    if i == 0:
                        dve.wait_ge(y_loaded, (self.b + db) * 16 + 16)
                    dve.wait_ge(stream_ready, self.stream.upto(name))
                    nc.vector.tensor_tensor(y[:, i, :], ring[self.stream.bank(name)][:, :], y[:, i, :], ALU.add)\
                        .then_inc(evacuated, 1)
                    dve.wait_ge(evacuated, self.stream.upto(name))
                    nc.vector.bn_stats(bn[:, i, :], y[:, i, :]).then_inc(bn_written, 1)

                def statistics(self, db, i):
                    dve.wait_ge(mask_ready, 1)
                    dve.wait_ge(bn_written, self.rows(db, i))
                    nc.vector.bn_aggr(mv[:, i, :], bn[:, i, :]).then_inc(moments, 1)
                    dve.wait_ge(moments, self.rows(db, i))
                    nc.vector.tensor_scalar_add(var_eps[:, i:i + 1], mv[:, i, 1:2], EPS_LN).then_inc(var_ready, 1)

                def normalise(self, db, i):
                    dve.wait_ge(rstd_ready, self.rows(db, i))
                    nc.vector.tensor_scalar(y[:, i, :], y[:, i, :], mv[:, i, 0:1], rstd[:, i:i + 1],
                                            ALU.subtract, ALU.mult).then_inc(y_done, 1)

            def until_zl(s):
                s.diagonals(0, gg_rows, 0.5, hsq, gg_diag)
                s.lo("zg", 1, 0, zg)
                s.exponents(0)
                s.lo("zg", 1, 1, zg)
                s.mask_ag(0, 0)
                s.mask_ag(0, 1)
                s.lo("zg", 1, 2, zg)
                s.mask_ag(0, 2)
                s.lo("zg", 1, 3, zg)
                s.mask_ag(0, 3)
                s.scale_of_ag(0)
                s.diagonals(0, gl_rows, 1.0, nsq, gl_diag)
                s.clamp_norms(0)
                s.lo("zl", 1, 0, zl)
                s.repeat_row("r", 0)
                s.lo("zl", 1, 1, zl)
                s.lo("zl", 1, 2, zl)
                s.mask_al(0, 0)
                s.mask_al(0, 1)
                s.lo("zl", 1, 3, zl)
                s.mask_al(0, 2)
                s.mask_al(0, 3)
                s.scale_of_al(0)

            def batch(b, parity, stream):
                s = Steps(b, stream)
                u_next = u[1 - parity]
                until_zl(s)
                s.lo("u", 1, 0, u_next)
                s.combine(0, 0)
                s.combine(0, 1)
                s.lo("u", 1, 1, u_next)
                s.combine(0, 2)
                s.combine(0, 3)
                s.lo("u", 1, 2, u_next)
                s.lo("kT", 0, 0, kT)
                x_transpose(b + 2, 0)
                s.lo("u", 1, 3, u_next)
                s.lo("kT", 0, 1, kT)
                for i in range(T):
                    if i + 1 < T:
                        x_transpose(b + 2, i + 1)
                    x_lo(b + 2, i)
                    s.residual(0, i)
                    if i + 2 < T:
                        s.lo("kT", 0, i + 2, kT)
                    s.statistics(0, i)
                    if i:
                        s.normalise(0, i - 1)
                s.normalise(0, T - 1)

            def last_two(b, stream):
                s = Steps(b, stream)
                until_zl(s)
                for i in range(T):
                    s.combine(0, i)
                s.diagonals(1, gg_rows, 0.5, hsq, gg_diag)
                s.lo("kT", 0, 0, kT)
                s.lo("kT", 0, 1, kT)
                s.residual(0, 0)
                s.statistics(0, 0)
                s.exponents(1)
                s.lo("kT", 0, 2, kT)
                s.normalise(0, 0)
                s.mask_ag(1, 0)
                s.residual(0, 1)
                s.lo("kT", 0, 3, kT)
                s.statistics(0, 1)
                s.mask_ag(1, 1)
                s.mask_ag(1, 2)
                s.residual(0, 2)
                s.statistics(0, 2)
                s.normalise(0, 1)
                s.mask_ag(1, 3)
                s.scale_of_ag(1)
                s.diagonals(1, gl_rows, 1.0, nsq, gl_diag)
                s.clamp_norms(1)
                s.normalise(0, 2)
                s.residual(0, 3)
                s.statistics(0, 3)
                s.repeat_row("r", 1)
                s.normalise(0, 3)
                s.lo("u", 1, 0, u[1])
                s.mask_al(1, 0)
                s.mask_al(1, 1)
                s.lo("u", 1, 1, u[1])
                s.mask_al(1, 2)
                s.mask_al(1, 3)
                s.scale_of_al(1)
                s.combine(1, 0)
                s.lo("u", 1, 2, u[1])
                for i in range(1, T):
                    s.combine(1, i)
                s.lo("u", 1, 3, u[1])
                s.lo("kT", 1, 0, kT)
                s.lo("kT", 1, 1, kT)
                for i in range(T):
                    s.residual(1, i)
                    if i + 2 < T:
                        s.lo("kT", 1, i + 2, kT)
                    s.statistics(1, i)
                    if i:
                        s.normalise(1, i - 1)
                s.normalise(1, T - 1)

            all_batches(dve, batch, last_two)

        @block.gpsimd
        def _(pool):
            nc.gpsimd.memset(ident[:, :], 0.0).then_inc(ident_cleared, 1)
            nc.gpsimd.memset(neg_half[:, :], -0.5).then_inc(neg_half_ready, 1)
            pool.wait_ge(ident_cleared, 1)
            nc.gpsimd.affine_select(out=ident[:, :], in_=ident[:, :], compare_op=ALU.not_equal, fill=1.0, base=0,
                                    pattern=[[-1, P]], channel_multiplier=1).then_inc(ident_ready, 1)
            pool.wait_ge(adj_loaded, 16)
            nc.gpsimd.affine_select(out=mask[:, :, :], in_=mask[:, :, :], compare_op=ALU.not_equal, fill=0.0,
                                    base=0, pattern=[[P, T], [-1, N]], channel_multiplier=1).then_inc(mask_ready, 1)
            pool.wait_ge(neg_half_ready, 1)
            pool.wait_ge(mask_ready, 1)

            def inverse_norms(b):
                pool.wait_ge(r_clamped, b + 1)
                nc.gpsimd.tensor_tensor(r[:, :], nsq_max[:, :], neg_half[:, :], ALU.pow).then_inc(r_ready, 1)

            def scale_mask(stream, db):
                pool.wait_ge(evacuated, stream.upto(("r", db, 0)))
                for i in range(T):
                    nc.gpsimd.tensor_tensor(mask_r[:, i, :], mask[:, i, :], row[:, :], ALU.mult)\
                        .then_inc(mask_r_ready, 1)

            def inverse_deviations(b):
                for i in range(T):
                    pool.wait_ge(var_ready, b * T + (i + 1))
                    nc.gpsimd.tensor_tensor(rstd[:, i:i + 1], var_eps[:, i:i + 1], neg_half[:, 0:1], ALU.pow)\
                        .then_inc(rstd_ready, 1)

            def batch(b, parity, stream):
                inverse_norms(b)
                scale_mask(stream, 0)
                inverse_deviations(b)

            def last_two(b, stream):
                inverse_norms(b)
                scale_mask(stream, 0)
                for i in range(T - 1):
                    pool.wait_ge(var_ready, b * T + (i + 1))
                    nc.gpsimd.tensor_tensor(rstd[:, i:i + 1], var_eps[:, i:i + 1], neg_half[:, 0:1], ALU.pow)\
                        .then_inc(rstd_ready, 1)
                inverse_norms(b + 1)
                pool.wait_ge(var_ready, b * T + T)
                nc.gpsimd.tensor_tensor(rstd[:, T - 1:T], var_eps[:, T - 1:T], neg_half[:, 0:1], ALU.pow)\
                    .then_inc(rstd_ready, 1)
                scale_mask(stream, 1)
                inverse_deviations(b + 1)

            all_batches(pool, batch, last_two)


_INS = ["x", "adj", "L0_gnn_W_lang", "L0_gnn_W_grav", "L0_gnn_W_V", "L0_gnn_W_O", "L0_gnn_gate_logit",
        "L0_gnn_log_sigma"]


def kernel(**inputs):
    import numpy as _np
    import concourse.bacc as _bacc
    from concourse import mybir as _mybir
    from concourse.bass_utils import run_bass_kernel_spmd as _run

    nc = _bacc.Bacc("TRN2", target_bir_lowering=False, num_devices=1)
    arrays, args = {}, []
    for name in _INS:
        a = _np.ascontiguousarray(inputs[name])
        if a.ndim < 2:
            a = a.reshape(1, 1)
        arrays[f"in_{name}_dram"] = a
        args.append(nc.dram_tensor(f"in_{name}_dram", a.shape, _mybir.dt.from_np(a.dtype), kind="ExternalInput").ap())
    shape = arrays["in_x_dram"].shape
    args.append(nc.dram_tensor("out_0_dram", shape, _mybir.dt.float32, kind="ExternalOutput").ap())
    graph_attention(nc, *args)
    r = _run(nc, [arrays], core_ids=[0])
    return r.results[0]["out_0_dram"]
```

```python
from contextlib import ExitStack

import concourse.bass as bass
from concourse import mybir

ALU = mybir.AluOpType
ACT = mybir.ActivationFunctionType
F32 = mybir.dt.float32
F32R = mybir.dt.float32r

P = 128
EPS_DEG = 1e-8
EPS_NORM = 1e-8
EPS_LN = 1e-5
RING = 4
Q = 32
WARM_UP = 10

G_BLOCKS = [(0, 1, 2), (1, 2, 3), (2, 3), (0, 3)]
OFF_BLOCKS = [(i, j) for i in range(4) for j in G_BLOCKS[i] if j != i]

START = [(kind, k) for k in range(4) for kind in ("xT", "wgT")] + [("wlT", k) for k in range(4)]
PROLOGUE = ([("zg", k) for k in range(4)] + [("zl", k) for k in range(3)] + [("wvo", k) for k in range(4)]
            + [("zl", 3)] + [("u", k) for k in range(4)])

BATCH = ([("zg", 1, 0), ("hsq", 0, 0), ("zg", 1, 1), ("zg", 1, 2), ("zg", 1, 3), ("zl", 1, 0), ("r", 0, 0),
          ("zl", 1, 1), ("zl", 1, 2), ("zl", 1, 3), ("u", 1, 0), ("u", 1, 1), ("u", 1, 2), ("kT", 0, 0),
          ("u", 1, 3), ("kT", 0, 1), ("out", 0, 0), ("kT", 0, 2), ("out", 0, 1), ("kT", 0, 3), ("out", 0, 2),
          ("out", 0, 3)])
LAST = (BATCH[:10]
        + [("u", 1, 0), ("kT", 0, 0), ("kT", 0, 1), ("out", 0, 0), ("hsq", 1, 0), ("kT", 0, 2), ("kT", 0, 3),
           ("out", 0, 1), ("out", 0, 2), ("r", 1, 0), ("u", 1, 1), ("u", 1, 2), ("u", 1, 3), ("kT", 1, 0),
           ("out", 0, 3), ("kT", 1, 1), ("out", 1, 0), ("kT", 1, 2), ("out", 1, 1), ("kT", 1, 3), ("out", 1, 2),
           ("out", 1, 3)])
SPLIT = ("zg", "zl", "u", "kT")


def splits(tiles):
    return [t for t in tiles if t[0] in SPLIT]


class Stream:

    def __init__(self, names, tiles, split, first):
        self.place = {t: n for n, t in enumerate(names)}
        self.place_split = {t: n for n, t in enumerate(splits(names))}
        self.tiles, self.split, self.first = tiles, split, first

    def number(self, name):
        return self.tiles + self.place[name]

    def upto(self, name):
        return self.tiles + (self.place[name] + 1)

    def split_upto(self, name):
        return self.split + (self.place_split[name] + 1)

    def bank(self, name):
        return (self.first + self.place[name]) % RING


def graph_attention(nc, x, adj, w_lang, w_grav, w_v, w_o, gate_logit, log_sigma, out):
    B, N, D = x.shape
    T = N // P
    QN = P // Q
    assert N == D == 4 * P and B >= 4 and B % 2 == 0
    n_pro = len(PROLOGUE)
    assert n_pro % RING == 0 and 2 * len(BATCH) % RING == 0

    x_rows = x.rearrange("b (t p) d -> b p t d", p=P)
    out_rows = out.rearrange("b (t p) d -> b t p d", p=P)
    x_blocks = x.rearrange("b (c j) (k a i) -> b a j k c i", j=Q, k=T, i=Q)
    w_o_blocks = w_o.rearrange("(c j) (k a i) -> a j k c i", j=Q, k=T, i=Q)

    def natural(w):
        return w.rearrange("(t p) d -> p t d", p=P)

    with ExitStack() as ctx:
        def sb(name, shape, dt=F32):
            return ctx.enter_context(nc.sbuf_tensor(name, shape, dt))

        def sem(name):
            return ctx.enter_context(nc.semaphore(name))

        def hi_lo(name):
            return sb(name + "_hi", [P, T, D], F32R), sb(name + "_lo", [P, T, D], F32R)

        wgT, wlT, wvo = hi_lo("wgT"), hi_lo("wlT"), hi_lo("wvo")
        xT, zg, zl, kT = hi_lo("xT"), hi_lo("zg"), hi_lo("zl"), hi_lo("kT")
        u = [hi_lo("u_even"), hi_lo("u_odd")]
        xb = sb("xb", [P, T, N])
        whole = sb("whole", [P, 2, N])
        y = sb("y", [P, T, D])
        ag = sb("ag", [P, T, N])
        al = sb("al", [P, T, N])
        mask = sb("mask", [P, T, N])
        mask_r = sb("mask_r", [P, T, N])
        off = sb("off", [P, len(OFF_BLOCKS), P])
        row = sb("row", [P, N])
        ident = sb("ident", [P, P])
        diag_out = sb("diag_out", [P, T, P], mybir.dt.bfloat16)
        hsq = sb("hsq", [P, T])
        nsq = sb("nsq", [P, T])
        wait_carrier = sb("wait_carrier", [P, 2, 2])
        hsq_wide = sb("hsq_wide", [P, P // T, T])
        r_wide = sb("r_wide", [P, P // T, T])
        nsq_max = sb("nsq_max", [P, T])
        r = sb("r", [P, T])
        sum_g = sb("sum_g", [P, T])
        sum_l = sb("sum_l", [P, T])
        deg = sb("deg", [P, 5, T])
        scale_g = sb("scale_g", [P, T])
        scale_l = sb("scale_l", [P, T])
        bn = sb("bn", [P, T, 6])
        mv = sb("mv", [P, T, 2])
        var_eps = sb("var_eps", [P, T])
        rstd = sb("rstd", [P, T])
        neg_half = sb("neg_half", [P, T])
        scal = sb("scal", [P, 12])
        gate_in, sig_in = scal[:, 0:1], scal[:, 1:2]
        gate_exp, sigma, gate_1p = scal[:, 2:3], scal[:, 3:4], scal[:, 4:5]
        w_l, w_g, sigma2, inv_sigma2 = scal[:, 5:6], scal[:, 6:7], scal[:, 7:8], scal[:, 8:9]
        wg_nat, wl_nat, wo_blocks, wv_nat, wv, woT = al, ag, mask_r, xb, u[1], kT
        y_last = xb

        g_bank = [ctx.enter_context(nc.psum_tensor(f"g_bank{i}", [P, N], F32)) for i in range(T)]
        ring = [ctx.enter_context(nc.psum_tensor(f"ring{i}", [P, N], F32)) for i in range(RING)]

        xb_loaded, y_loaded, stored = sem("xb_loaded"), sem("y_loaded"), sem("stored")
        y_last_loaded = sem("y_last_loaded")
        x0_loaded = [sem(f"x0_loaded{k}") for k in range(T)]
        wg_loaded = [sem(f"wg_loaded{k}") for k in range(T)]
        wl_loaded, wo_loaded, wv_loaded = sem("wl_loaded"), sem("wo_loaded"), sem("wv_loaded")
        adj_loaded, scalars_loaded = sem("adj_loaded"), sem("scalars_loaded")
        start_ready, start_hi, start_evacuated = sem("start_ready"), sem("start_hi"), sem("start_evacuated")
        ident_cleared, ident_ready, mask_ready = sem("ident_cleared"), sem("ident_ready"), sem("mask_ready")
        neg_half_ready, scalar_exps, scalar_step = sem("neg_half_ready"), sem("scalar_exps"), sem("scalar_step")
        wv_hi, wv_split = sem("wv_hi"), sem("wv_split")
        table_loaded = sem("table_loaded")
        whole_transposed, whole_hi, whole_split = sem("whole_transposed"), sem("whole_hi"), sem("whole_split")
        stream_ready, hi_written, evacuated = sem("stream_ready"), sem("hi_written"), sem("evacuated")
        gg_rows, gg_diag, gg_off, gg_full = sem("gg_rows"), sem("gg_diag"), sem("gg_off"), sem("gg_full")
        gl_rows, gl_diag, gl_off, gl_full = sem("gl_rows"), sem("gl_diag"), sem("gl_off"), sem("gl_full")
        r_clamped, r_ready, mask_r_ready = sem("r_clamped"), sem("r_ready"), sem("mask_r_ready")
        first_mask_r_ready = sem("first_mask_r_ready")
        hsq_widened, r_widened = sem("hsq_widened"), sem("r_widened")
        exp_arg, exp_done, ag_masked, ag_scaled = sem("exp_arg"), sem("exp_done"), sem("ag_masked"), sem("ag_scaled")
        al_masked, k_ready = sem("al_masked"), sem("k_ready")
        deg_step = sem("deg_step")
        DEG_G, DEG_ALL = 3, 7
        bn_written, moments, var_ready, rstd_ready, y_done = (
            sem("bn_written"), sem("moments"), sem("var_ready"), sem("rstd_ready"), sem("y_done"))

        block = ctx.enter_context(nc.Block())

        def all_batches(engine, batch, last_two):
            per, per_split = len(BATCH), len(splits(BATCH))
            with engine.Fori(0, (B - 2) // 2) as pair:
                for parity in range(2):
                    b = pair * 2 + parity
                    batch(b, parity, Stream(BATCH, b * per + n_pro, b * per_split + n_pro, parity * per % RING))
            b = B - 2
            last_two(b, Stream(LAST, b * per + n_pro, b * per_split + n_pro, 0))

        @block.sync
        def _(sp):
            def load_blocks(tile, blocks, loaded):
                for a in range(QN):
                    sp.dma_start(tile[a * Q:(a + 1) * Q, :, :].rearrange("j k (c i) -> j k c i", i=Q),
                                 blocks[a]).then_inc(loaded, 16)

            def store_rows(b, rows=y):
                for i in range(T):
                    sp.wait_ge(y_done, b * T + (i + 1))
                    sp.dma_start(out_rows[b][i], rows[:, i, :]).then_inc(stored, 16)

            def load_residual(b):
                sp.wait_ge(stored, b * (16 * T))
                sp.dma_start(y[:, :, :], x_rows[b]).then_inc(y_loaded, 16)

            for k in range(T):
                sp.dma_start(y[:, :, k * P:(k + 1) * P], x_rows[0][:, :, k * P:(k + 1) * P])\
                    .then_inc(x0_loaded[k], 16)
            sp.dma_start(wl_nat[:, :, :], natural(w_lang)).then_inc(wl_loaded, 16)
            sp.dma_start(wv_nat[:, :, :], natural(w_v)).then_inc(wv_loaded, 16)
            load_blocks(wo_blocks, w_o_blocks, wo_loaded)
            sp.dma_start(gate_in, gate_logit.to_broadcast([P, 1])).then_inc(scalars_loaded, 16)
            sp.dma_start(sig_in, log_sigma.to_broadcast([P, 1])).then_inc(scalars_loaded, 16)
            sp.dma_start(mask[:, :, :], natural(adj)).then_inc(adj_loaded, 16)
            sp.wait_ge(wv_split, T)
            load_blocks(xb, x_blocks[1], xb_loaded)

            def batch(b, parity, stream):
                sp.wait_ge(whole_transposed, b * T + 2 * T)
                load_blocks(xb, x_blocks[b + 2], xb_loaded)
                store_rows(b)
                load_residual(b + 1)

            def last_two(b, stream):
                sp.wait_ge(whole_transposed, b * T + 2 * T)
                sp.dma_start(y_last[:, :, :], x_rows[b + 1]).then_inc(y_last_loaded, 16)
                store_rows(b)
                store_rows(b + 1, y_last)

            all_batches(sp, batch, last_two)
            sp.wait_ge(stored, 16 * T * B)

        @block.tensor
        def _(pe):
            def claim_bank(n):
                if not isinstance(n, int) or n >= RING:
                    pe.wait_ge(evacuated, n - (RING - 1))

            def transposed(bank, blocks):
                for j, blk in enumerate(blocks):
                    last = nc.tensor.transpose(bank[:, j * P:(j + 1) * P], blk, ident[:, :])
                return last

            def product_step(psum, left, right, k):
                (lh, ll), (rh, rl) = left(k), right(k)
                nc.tensor.matmul(psum, lh, rh, start=k == 0, stop=False)
                nc.tensor.matmul(psum, lh, rl, start=False, stop=False)
                return nc.tensor.matmul(psum, ll, rh, start=False, stop=k == T - 1)

            def product(psum, left, right):
                for k in range(T):
                    last = product_step(psum, left, right, k)
                return last

            def column_block(pair, i):
                return lambda k: tuple(t[:, k, i * P:(i + 1) * P] for t in pair)

            def whole_row(pair):
                return lambda k: tuple(t[:, k, :] for t in pair)

            def project(bank, kind, i):
                if kind == "zg":
                    last = product(bank[:, :], column_block(wgT, i), whole_row(xT))
                elif kind == "zl":
                    last = product(bank[:, :], column_block(wlT, i), whole_row(xT))
                else:
                    last = product(bank[:, :], column_block(xT, i), whole_row(wvo))
                last.then_inc(stream_ready, 1)

            def gram_row(z, i, rows_done):
                step = G_BLOCKS[i][1] - G_BLOCKS[i][0]
                cols = slice(G_BLOCKS[i][0], G_BLOCKS[i][-1] + 1, step)
                psum = g_bank[i][:, :].rearrange("p (c n) -> p c n", n=P)[:, cols, :]
                right = [t[:, :, :].rearrange("p k (c n) -> p k c n", n=P) for t in z]
                product(psum, column_block(z, i), lambda k: tuple(t[:, k, cols, :] for t in right))\
                    .then_inc(rows_done, 1)

            def mirror(full):
                for s, (i, j) in enumerate(OFF_BLOCKS):
                    last = nc.tensor.transpose(g_bank[j][:, i * P:(i + 1) * P], off[:, s, :], ident[:, :])
                last.then_inc(full, 1)

            pe.wait_ge(ident_ready, 1)
            for _ in range(WARM_UP):
                nc.tensor.transpose(g_bank[0][:, 0:P], ident[:, :], ident[:, :])

            def start_tile(kind, k):
                n = START.index((kind, k))
                if n >= T:
                    pe.wait_ge(start_evacuated, n - (T - 1))
                if kind == "xT":
                    pe.wait_ge(x0_loaded[k], 16)
                elif kind == "wgT":
                    pe.wait_ge(wg_loaded[k], 16)
                elif k == 0:
                    pe.wait_ge(wl_loaded, 16)
                src = {"xT": y, "wgT": wg_nat, "wlT": wl_nat}[kind]
                transposed(g_bank[n % T], [src[:, j, k * P:(k + 1) * P] for j in range(T)]).then_inc(start_ready, 1)

            def start_zg_step(k):
                pe.wait_ge(start_evacuated, START.index(("wgT", k)) + 1)
                for i in range(T):
                    last = product_step(ring[i][:, :], column_block(wgT, i), whole_row(xT), k)
                    if k == T - 1:
                        last.then_inc(stream_ready, 1)

            for kind, k in START[:4]:
                start_tile(kind, k)
            start_zg_step(0)
            for k in range(1, T - 1):
                start_tile("xT", k + 1)
                start_tile("wgT", k + 1)
                start_zg_step(k)
            for k in range(T):
                start_tile("wlT", k)
            start_zg_step(T - 1)
            for n, (kind, i) in enumerate(PROLOGUE):
                if kind == "zg":
                    continue
                bank = ring[n % RING]
                claim_bank(n)
                if (kind, i) == ("zl", 0):
                    pe.wait_ge(start_evacuated, len(START))
                elif (kind, i) == ("wvo", 0):
                    pe.wait_ge(wv_split, T)
                    pe.wait_ge(whole_split, T)
                elif (kind, i) == ("u", 0):
                    pe.wait_ge(evacuated, PROLOGUE.index(("wvo", T - 1)) + 1)
                if kind == "wvo":
                    product(bank[:, :], column_block(wv, i), whole_row(woT)).then_inc(stream_ready, 1)
                else:
                    project(bank, kind, i)

            class Steps:

                def __init__(self, b, stream):
                    self.b, self.stream = b, stream

                def begin(self, name):
                    claim_bank(self.stream.number(name))
                    return ring[self.stream.bank(name)]

                def gram_g(self, db, row_tiles=range(T)):
                    for i in row_tiles:
                        gram_row(zg, i, gg_rows)

                def gram_l(self, db):
                    for i in range(T):
                        pe.wait_ge(exp_arg, (self.b + db) * T + (i + 1))
                        gram_row(zl, i, gl_rows)

                def mirror_g(self, db):
                    pe.wait_ge(gg_off, (self.b + db) * T + T)
                    mirror(gg_full)
                    pe.wait_ge(hsq_widened, (self.b + db) + 1)
                    self.column_as_rows("hsq", db, hsq_wide)

                def mirror_l(self, db):
                    pe.wait_ge(gl_off, (self.b + db) * T + T)
                    mirror(gl_full)

                def r_as_rows(self, db):
                    pe.wait_ge(r_widened, (self.b + db) + 1)
                    self.column_as_rows("r", db, r_wide)

                def column_as_rows(self, kind, db, wide):
                    bank = self.begin((kind, db, 0))
                    nc.tensor.transpose(bank[:, 0:P], wide[:, :, :].rearrange("p s t -> p (s t)"), ident[:, :])\
                        .then_inc(stream_ready, 1)

                def project(self, kind, i):
                    bank = self.begin((kind, 1, i))
                    if (kind, i) == ("zg", 0):
                        pe.wait_ge(whole_split, self.b * T + 2 * T)
                    project(bank, kind, i)

                def transpose_k(self, db, i):
                    bank = self.begin(("kT", db, i))
                    pe.wait_ge(k_ready, (self.b + db) * T + (i + 1))
                    transposed(bank, [al[:, i, j * P:(j + 1) * P] for j in range(T)]).then_inc(stream_ready, 1)

                def aggregate(self, db, i, parity):
                    bank = self.begin(("out", db, i))
                    pe.wait_ge(evacuated, self.stream.upto(("kT", db, i)))
                    kT_i = [t[:, i, :].rearrange("p (k n) -> p k n", n=P) for t in kT]
                    product(bank[:, :], lambda k: tuple(t[:, k, :] for t in kT_i), whole_row(u[parity]))\
                        .then_inc(stream_ready, 1)

            def batch(b, parity, stream):
                s = Steps(b, stream)
                s.gram_g(0)
                s.project("zg", 0)
                s.mirror_g(0)
                for i in range(1, T):
                    s.project("zg", i)
                s.gram_l(0)
                s.project("zl", 0)
                s.mirror_l(0)
                s.r_as_rows(0)
                for i in range(1, T):
                    s.project("zl", i)
                for i in range(3):
                    s.project("u", i)
                s.transpose_k(0, 0)
                s.project("u", 3)
                s.transpose_k(0, 1)
                for i in range(T):
                    s.aggregate(0, i, parity)
                    if i + 2 < T:
                        s.transpose_k(0, i + 2)

            def last_two(b, stream):
                s = Steps(b, stream)
                s.gram_g(0)
                s.project("zg", 0)
                s.mirror_g(0)
                for i in range(1, T):
                    s.project("zg", i)
                s.gram_l(0)
                s.project("zl", 0)
                s.mirror_l(0)
                s.r_as_rows(0)
                for i in range(1, T):
                    s.project("zl", i)
                s.project("u", 0)
                pe.wait_ge(evacuated, stream.upto(("zg", 1, T - 1)))
                pe.wait_ge(al_masked, b * T + T)
                s.gram_g(1, range(T - 1))
                s.transpose_k(0, 0)
                s.gram_g(1, [T - 1])
                s.transpose_k(0, 1)
                s.aggregate(0, 0, 0)
                s.mirror_g(1)
                s.transpose_k(0, 2)
                s.transpose_k(0, 3)
                s.aggregate(0, 1, 0)
                s.gram_l(1)
                s.aggregate(0, 2, 0)
                s.r_as_rows(1)
                s.mirror_l(1)
                s.project("u", 1)
                s.project("u", 2)
                s.project("u", 3)
                s.transpose_k(1, 0)
                s.aggregate(0, 3, 0)
                s.transpose_k(1, 1)
                pe.wait_ge(evacuated, stream.upto(("u", 1, T - 1)))
                for i in range(T):
                    s.aggregate(1, i, 1)
                    if i + 2 < T:
                        s.transpose_k(1, i + 2)

            all_batches(pe, batch, last_two)

        @block.scalar
        def _(act):
            act.wait_ge(neg_half_ready, 1)
            nc.scalar.activation(gate_1p, neg_half[:, 0:1], ACT.Exp).then_inc(table_loaded, 1)

            for k in range(T):
                act.dma_start(wg_nat[:, :, k * P:(k + 1) * P], natural(w_grav)[:, :, k * P:(k + 1) * P])\
                    .then_inc(wg_loaded[k], 16)

            def split_hi(bank, ready, pair, i):
                act.wait_ge(stream_ready, ready)
                nc.scalar.activation(pair[0][:, i, :], bank[:, :], ACT.Copy).then_inc(hi_written, 1)

            def whole_hi_part(b, k, pair):
                act.wait_ge(whole_transposed, b * T + (k + 1))
                nc.scalar.activation(pair[0][:, k, :], whole[:, k % 2, :], ACT.Copy).then_inc(whole_hi, 1)

            for n, (kind, k) in enumerate(START):
                act.wait_ge(start_ready, n + 1)
                nc.scalar.activation({"xT": xT, "wgT": wgT, "wlT": wlT}[kind][0][:, k, :], g_bank[n % T][:, :],
                                     ACT.Copy).then_inc(start_hi, 1)
            for n, (kind, i) in enumerate(PROLOGUE):
                split_hi(ring[n % RING], n + 1, {"zg": zg, "zl": zl, "wvo": wvo, "u": u[0]}[kind], i)
                if (kind, i) == ("zg", T - 1):
                    act.wait_ge(wv_loaded, 16)
                    for k in range(T):
                        nc.scalar.activation(wv[0][:, k, :], wv_nat[:, k, :], ACT.Copy).then_inc(wv_hi, 1)
                        if k:
                            whole_hi_part(0, k - 1, woT)
                    whole_hi_part(0, T - 1, woT)
                    act.wait_ge(scalars_loaded, 32)
                    nc.scalar.activation(gate_exp, gate_in, ACT.Exp, scale=-1.0).then_inc(scalar_exps, 1)
                    nc.scalar.activation(sigma, sig_in, ACT.Exp).then_inc(scalar_exps, 1)
            for k in range(T):
                whole_hi_part(1, k, xT)
            act.wait_ge(scalar_step, 5)

            class Steps:

                def __init__(self, b, stream):
                    self.b, self.stream = b, stream

                def hi(self, kind, db, i, pair):
                    name = (kind, db, i)
                    split_hi(ring[self.stream.bank(name)], self.stream.upto(name), pair, i)

                def copy_off(self, db, diag_read, done, row_tiles=range(T)):
                    for i in row_tiles:
                        mine = [s for s, (a, _) in enumerate(OFF_BLOCKS) if a == i]
                        j0 = OFF_BLOCKS[mine[0]][1]
                        act.wait_ge(diag_read, (self.b + db) * T + (i + 1))
                        nc.scalar.activation(off[:, mine[0]:mine[-1] + 1, :],
                                             g_bank[i][:, j0 * P:(j0 + len(mine)) * P]
                                             .rearrange("p (c n) -> p c n", n=P), ACT.Copy).then_inc(done, 1)

                def widen(self, db, ready, count, col, wide, done):
                    act.wait_ge(ready, count)
                    nc.scalar.activation(wide[:, :, :], col[:, :].unsqueeze(1).to_broadcast([P, P // T, T]),
                                         ACT.Copy).then_inc(done, 1)

                def widen_hsq(self, db):
                    self.widen(db, gg_diag, (self.b + db) * T + T, hsq, hsq_wide, hsq_widened)

                def widen_r(self, db):
                    self.widen(db, r_ready, (self.b + db) + 1, r, r_wide, r_widened)

                def exp(self, db, i):
                    act.wait_ge(exp_arg, (self.b + db) * T + (i + 1))
                    nc.scalar.activation(ag[:, i, :], ag[:, i, :], ACT.Exp, scale=inv_sigma2).then_inc(exp_done, 1)

                def scale_ag(self, db):
                    act.wait_ge(deg_step, (self.b + db) * DEG_ALL + DEG_G)
                    for i in range(T):
                        nc.scalar.activation(ag[:, i, :], ag[:, i, :], ACT.Copy, scale=scale_g[:, i:i + 1])\
                            .then_inc(ag_scaled, 1)

            def until_zl(s):
                s.copy_off(0, gg_diag, gg_off)
                s.widen_hsq(0)
                s.hi("zg", 1, 0, zg)
                s.exp(0, 0)
                s.hi("zg", 1, 1, zg)
                s.exp(0, 1)
                s.exp(0, 2)
                s.hi("zg", 1, 2, zg)
                s.exp(0, 3)
                s.hi("zg", 1, 3, zg)
                s.copy_off(0, gl_diag, gl_off)
                s.widen_r(0)
                s.hi("zl", 1, 0, zl)
                s.hi("zl", 1, 1, zl)
                s.scale_ag(0)
                s.hi("zl", 1, 2, zl)
                s.hi("zl", 1, 3, zl)

            def batch(b, parity, stream):
                s = Steps(b, stream)
                until_zl(s)
                for i in range(3):
                    s.hi("u", 1, i, u[1 - parity])
                s.hi("kT", 0, 0, kT)
                s.hi("u", 1, 3, u[1 - parity])
                s.hi("kT", 0, 1, kT)
                for k in range(T):
                    whole_hi_part(b + 2, k, xT)
                    if k + 2 < T:
                        s.hi("kT", 0, k + 2, kT)

            def last_two(b, stream):
                s = Steps(b, stream)
                until_zl(s)
                s.hi("u", 1, 0, u[1])
                s.copy_off(1, gg_diag, gg_off, range(T - 1))
                s.hi("kT", 0, 0, kT)
                s.copy_off(1, gg_diag, gg_off, [T - 1])
                s.widen_hsq(1)
                s.hi("kT", 0, 1, kT)
                s.hi("kT", 0, 2, kT)
                s.hi("kT", 0, 3, kT)
                for i in range(T):
                    s.exp(1, i)
                s.copy_off(1, gl_diag, gl_off)
                s.widen_r(1)
                s.scale_ag(1)
                s.hi("u", 1, 1, u[1])
                s.hi("u", 1, 2, u[1])
                s.hi("u", 1, 3, u[1])
                s.hi("kT", 1, 0, kT)
                for i in range(1, T):
                    s.hi("kT", 1, i, kT)

            all_batches(act, batch, last_two)

        @block.vector
        def _(dve):
            def split_lo(bank, hi_count, pair, i):
                dve.wait_ge(hi_written, hi_count)
                nc.vector.tensor_tensor(pair[1][:, i, :], bank[:, :], pair[0][:, i, :].bitcast(F32),
                                        ALU.subtract).then_inc(evacuated, 1)

            def whole_transpose(b, k, blocks):
                if k >= 2:
                    dve.wait_ge(whole_split, b * T + (k - 1))
                elif not isinstance(b, int) or b > 0:
                    dve.wait_ge(whole_split, (b - 1) * T + (k + 3))
                nc.vector.transpose(whole[:, k % 2, :], blocks[:, k, :]).then_inc(whole_transposed, 1)

            def whole_lo_part(b, k, pair):
                dve.wait_ge(whole_hi, b * T + (k + 1))
                nc.vector.tensor_tensor(pair[1][:, k, :], whole[:, k % 2, :], pair[0][:, k, :].bitcast(F32),
                                        ALU.subtract).then_inc(whole_split, 1)

            def x_transpose(b, k):
                if k == 0:
                    dve.wait_ge(xb_loaded, b * (16 * QN))
                whole_transpose(b, k, xb)

            for n, (kind, k) in enumerate(START):
                pair = {"xT": xT, "wgT": wgT, "wlT": wlT}[kind]
                dve.wait_ge(start_hi, n + 1)
                nc.vector.tensor_tensor(pair[1][:, k, :], g_bank[n % T][:, :], pair[0][:, k, :].bitcast(F32),
                                        ALU.subtract).then_inc(start_evacuated, 1)
            for n, (kind, i) in enumerate(PROLOGUE):
                if (kind, i) == ("u", 2):
                    x_transpose(1, 0)
                    x_transpose(1, 1)
                split_lo(ring[n % RING], n + 1, {"zg": zg, "zl": zl, "wvo": wvo, "u": u[0]}[kind], i)
                if (kind, i) == ("zg", T - 1):
                    dve.wait_ge(wo_loaded, 16 * QN)
                    whole_transpose(0, 0, wo_blocks)
                    whole_transpose(0, 1, wo_blocks)
                    for k in range(T):
                        whole_lo_part(0, k, woT)
                        if k + 2 < T:
                            whole_transpose(0, k + 2, wo_blocks)
                if (kind, i) == ("zl", 0):
                    dve.wait_ge(table_loaded, 1)
                    dve.wait_ge(scalar_exps, 2)
                    nc.vector.tensor_scalar_add(gate_1p, gate_exp, 1.0).then_inc(scalar_step, 1)
                    nc.vector.tensor_tensor(sigma2, sigma, sigma, ALU.mult).then_inc(scalar_step, 1)
                    dve.wait_ge(scalar_step, 2)
                    nc.vector.reciprocal(w_l, gate_1p).then_inc(scalar_step, 1)
                    nc.vector.reciprocal(inv_sigma2, sigma2).then_inc(scalar_step, 1)
                    dve.wait_ge(scalar_step, 4)
                    nc.vector.tensor_scalar(w_g, w_l, -1.0, 1.0, ALU.mult, ALU.add).then_inc(scalar_step, 1)
            for k in range(T):
                whole_lo_part(1, k, xT)
                if k + 2 < T:
                    x_transpose(1, k + 2)
            dve.wait_ge(scalar_step, 5)
            dve.wait_ge(ident_ready, 1)
            dve.wait_ge(mask_ready, 1)

            class Steps:

                def __init__(self, b, stream):
                    self.b, self.stream = b, stream

                def rows(self, db, i):
                    return (self.b + db) * T + (i + 1)

                def lo(self, kind, db, i, pair):
                    name = (kind, db, i)
                    split_lo(ring[self.stream.bank(name)], self.stream.split_upto(name), pair, i)

                def diagonals(self, db, rows_done, factor, col, done, row_tiles=range(T)):
                    for i in row_tiles:
                        dve.wait_ge(rows_done, self.rows(db, i))
                        nc.vector.scalar_tensor_tensor(
                            out=diag_out[:, i, :], in0=g_bank[i][:, i * P:(i + 1) * P], scalar=factor,
                            in1=ident[:, :], op0=ALU.mult, op1=ALU.mult, accum_out=col[:, i:i + 1])\
                            .then_inc(done, 1)

                def repeat_row(self, kind, db):
                    bank = ring[self.stream.bank((kind, db, 0))]
                    dve.wait_ge(stream_ready, self.stream.upto((kind, db, 0)))
                    nc.vector.memset(wait_carrier[:, ("hsq", "r").index(kind)], 0.0)
                    for t in range(T):
                        last = nc.vector.stream_shuffle(row[:, t * P:(t + 1) * P], bank[:, 0:P], [t] * Q)
                    last.then_inc(evacuated, 1)

                def exponent(self, db, i):
                    nc.vector.scalar_tensor_tensor(
                        out=ag[:, i, :], in0=g_bank[i][:, :], scalar=hsq[:, i:i + 1], in1=row[:, :],
                        op0=ALU.subtract, op1=ALU.subtract).then_inc(exp_arg, 1)

                def exponents_row(self, db):
                    self.repeat_row("hsq", db)
                    dve.wait_ge(gg_full, (self.b + db) + 1)
                    dve.wait_ge(evacuated, self.stream.upto(("hsq", db, 0)))

                def mask_ag(self, db, i):
                    dve.wait_ge(exp_done, self.rows(db, i))
                    nc.vector.scalar_tensor_tensor(
                        out=ag[:, i, :], in0=ag[:, i, :], scalar=1.0, in1=mask[:, i, :],
                        op0=ALU.min, op1=ALU.mult, accum_out=sum_g[:, i:i + 1]).then_inc(ag_masked, 1)

                def scale_of_ag(self, db):
                    dve.wait_ge(ag_masked, self.rows(db, T - 1))
                    step = (self.b + db) * DEG_ALL
                    nc.vector.tensor_scalar_max(deg[:, 0, :], sum_g[:, :], EPS_DEG).then_inc(deg_step, 1)
                    dve.wait_ge(deg_step, step + 1)
                    nc.vector.reciprocal(deg[:, 1, :], deg[:, 0, :]).then_inc(deg_step, 1)
                    dve.wait_ge(deg_step, step + 2)
                    nc.vector.tensor_scalar_mul(scale_g[:, :], deg[:, 1, :], w_g).then_inc(deg_step, 1)

                def clamp_norms(self, db):
                    dve.wait_ge(gl_diag, self.rows(db, T - 1))
                    nc.vector.tensor_scalar_max(nsq_max[:, :], nsq[:, :], EPS_NORM * EPS_NORM)\
                        .then_inc(r_clamped, 1)

                def scale_first_mask(self, db):
                    dve.wait_ge(evacuated, self.stream.upto(("r", db, 0)))
                    nc.vector.tensor_tensor(mask_r[:, 0, :], mask[:, 0, :], row[:, :], ALU.mult)\
                        .then_inc(first_mask_r_ready, 1)

                def mask_al(self, db, i):
                    if i == 0:
                        dve.wait_ge(gl_full, (self.b + db) + 1)
                    if db == 0:
                        dve.wait_ge(mask_r_ready, self.rows(0, i))
                    elif i == 0:
                        dve.wait_ge(first_mask_r_ready, 1)
                    else:
                        dve.wait_ge(mask_r_ready, (self.b + db) * T + i)
                    nc.vector.scalar_tensor_tensor(
                        out=al[:, i, :], in0=g_bank[i][:, :], scalar=0.0, in1=mask_r[:, i, :],
                        op0=ALU.max, op1=ALU.mult, accum_out=sum_l[:, i:i + 1]).then_inc(al_masked, 1)

                def scale_of_al(self, db, first=0, end=T, earlier=0):
                    dve.wait_ge(al_masked, self.rows(db, end - 1))
                    step = (self.b + db) * DEG_ALL + (earlier * (DEG_ALL - DEG_G))
                    c = slice(first, end)
                    nc.vector.tensor_tensor(deg[:, 2, c], sum_l[:, c], r[:, c], ALU.mult).then_inc(deg_step, 1)
                    dve.wait_ge(deg_step, step + 4)
                    nc.vector.tensor_scalar_max(deg[:, 3, c], deg[:, 2, c], EPS_DEG).then_inc(deg_step, 1)
                    dve.wait_ge(deg_step, step + 5)
                    nc.vector.reciprocal(deg[:, 4, c], deg[:, 3, c]).then_inc(deg_step, 1)
                    dve.wait_ge(deg_step, step + 6)
                    nc.vector.scalar_tensor_tensor(out=scale_l[:, c], in0=deg[:, 4, c], scalar=w_l, in1=r[:, c],
                                                   op0=ALU.mult, op1=ALU.mult).then_inc(deg_step, 1)
                    dve.wait_ge(deg_step, step + 7)

                def combine(self, db, i):
                    dve.wait_ge(ag_scaled, self.rows(db, i))
                    nc.vector.scalar_tensor_tensor(
                        out=al[:, i, :], in0=al[:, i, :], scalar=scale_l[:, i:i + 1], in1=ag[:, i, :],
                        op0=ALU.mult, op1=ALU.add).then_inc(k_ready, 1)

                def y(self, db):
                    return y_last if db else y

                def residual(self, db, i):
                    name, y_b = ("out", db, i), self.y(db)
                    if i == 0:
                        if db:
                            dve.wait_ge(y_last_loaded, 16)
                        else:
                            dve.wait_ge(y_loaded, self.b * 16)
                    dve.wait_ge(stream_ready, self.stream.upto(name))
                    nc.vector.tensor_tensor(y_b[:, i, :], ring[self.stream.bank(name)][:, :], y_b[:, i, :], ALU.add)\
                        .then_inc(evacuated, 1)

                def row_sums(self, db, i):
                    y_b = self.y(db)
                    dve.wait_ge(evacuated, self.stream.upto(("out", db, i)))
                    nc.vector.bn_stats(bn[:, i, :], y_b[:, i, :]).then_inc(bn_written, 1)

                def statistics(self, db, i):
                    dve.wait_ge(mask_ready, 1)
                    dve.wait_ge(bn_written, self.rows(db, i))
                    nc.vector.bn_aggr(mv[:, i, :], bn[:, i, :]).then_inc(moments, 1)
                    dve.wait_ge(moments, self.rows(db, i))
                    nc.vector.tensor_scalar_add(var_eps[:, i:i + 1], mv[:, i, 1:2], EPS_LN).then_inc(var_ready, 1)

                def normalise(self, db, i):
                    dve.wait_ge(rstd_ready, self.rows(db, i))
                    nc.vector.tensor_scalar(self.y(db)[:, i, :], self.y(db)[:, i, :], mv[:, i, 0:1], rstd[:, i:i + 1],
                                            ALU.subtract, ALU.mult).then_inc(y_done, 1)

            def until_zl(s):
                s.diagonals(0, gg_rows, 0.5, hsq, gg_diag)
                s.lo("zg", 1, 0, zg)
                s.exponents_row(0)
                for i in range(T):
                    s.exponent(0, i)
                s.lo("zg", 1, 1, zg)
                s.mask_ag(0, 0)
                s.mask_ag(0, 1)
                s.lo("zg", 1, 2, zg)
                s.mask_ag(0, 2)
                s.lo("zg", 1, 3, zg)
                s.mask_ag(0, 3)
                s.scale_of_ag(0)
                s.diagonals(0, gl_rows, 1.0, nsq, gl_diag)
                s.clamp_norms(0)
                s.lo("zl", 1, 0, zl)
                s.repeat_row("r", 0)
                s.lo("zl", 1, 1, zl)
                s.lo("zl", 1, 2, zl)
                s.mask_al(0, 0)
                s.mask_al(0, 1)
                s.lo("zl", 1, 3, zl)
                s.mask_al(0, 2)
                s.mask_al(0, 3)
                s.scale_of_al(0)

            def batch(b, parity, stream):
                s = Steps(b, stream)
                u_next = u[1 - parity]
                until_zl(s)
                s.lo("u", 1, 0, u_next)
                s.combine(0, 0)
                s.combine(0, 1)
                s.lo("u", 1, 1, u_next)
                s.combine(0, 2)
                s.combine(0, 3)
                s.lo("u", 1, 2, u_next)
                s.lo("kT", 0, 0, kT)
                x_transpose(b + 2, 0)
                s.lo("u", 1, 3, u_next)
                s.lo("kT", 0, 1, kT)
                for i in range(T):
                    if i + 1 < T:
                        x_transpose(b + 2, i + 1)
                    whole_lo_part(b + 2, i, xT)
                    s.residual(0, i)
                    s.row_sums(0, i)
                    if i + 2 < T:
                        s.lo("kT", 0, i + 2, kT)
                    s.statistics(0, i)
                    if i:
                        s.normalise(0, i - 1)
                s.normalise(0, T - 1)

            def last_two(b, stream):
                s = Steps(b, stream)
                until_zl(s)
                s.lo("u", 1, 0, u[1])
                for i in range(T):
                    s.combine(0, i)
                s.diagonals(1, gg_rows, 0.5, hsq, gg_diag, range(T - 1))
                s.lo("kT", 0, 0, kT)
                s.diagonals(1, gg_rows, 0.5, hsq, gg_diag, [T - 1])
                s.lo("kT", 0, 1, kT)
                s.residual(0, 0)
                s.row_sums(0, 0)
                s.exponents_row(1)
                s.exponent(1, 0)
                s.lo("kT", 0, 2, kT)
                s.exponent(1, 1)
                s.lo("kT", 0, 3, kT)
                s.exponent(1, 2)
                s.exponent(1, 3)
                s.statistics(0, 0)
                s.mask_ag(1, 0)
                s.residual(0, 1)
                s.row_sums(0, 1)
                s.mask_ag(1, 1)
                s.normalise(0, 0)
                s.statistics(0, 1)
                s.mask_ag(1, 2)
                s.diagonals(1, gl_rows, 1.0, nsq, gl_diag)
                s.clamp_norms(1)
                s.mask_ag(1, 3)
                s.scale_of_ag(1)
                s.normalise(0, 1)
                s.residual(0, 2)
                s.repeat_row("r", 1)
                s.scale_first_mask(1)
                s.mask_al(1, 0)
                s.scale_of_al(1, end=1)
                s.combine(1, 0)
                s.lo("u", 1, 1, u[1])
                s.mask_al(1, 1)
                s.mask_al(1, 2)
                s.row_sums(0, 2)
                s.lo("u", 1, 2, u[1])
                s.mask_al(1, 3)
                s.scale_of_al(1, first=1, earlier=1)
                s.combine(1, 1)
                s.combine(1, 2)
                s.lo("u", 1, 3, u[1])
                s.lo("kT", 1, 0, kT)
                s.combine(1, 3)
                s.residual(0, 3)
                s.lo("kT", 1, 1, kT)
                s.row_sums(0, 3)
                s.statistics(0, 2)
                s.statistics(0, 3)
                s.normalise(0, 2)
                s.normalise(0, 3)
                for i in range(T):
                    s.residual(1, i)
                    s.row_sums(1, i)
                    if i + 2 < T:
                        s.lo("kT", 1, i + 2, kT)
                    s.statistics(1, i)
                    if i:
                        s.normalise(1, i - 1)
                s.normalise(1, T - 1)

            all_batches(dve, batch, last_two)

        @block.gpsimd
        def _(pool):
            nc.gpsimd.memset(neg_half[:, :], -0.5).then_inc(neg_half_ready, 1)
            nc.gpsimd.memset(ident[:, :], 0.0).then_inc(ident_cleared, 1)
            pool.wait_ge(ident_cleared, 1)
            nc.gpsimd.affine_select(out=ident[:, :], in_=ident[:, :], compare_op=ALU.not_equal, fill=1.0, base=0,
                                    pattern=[[-1, P]], channel_multiplier=1).then_inc(ident_ready, 1)
            for k in range(T):
                pool.wait_ge(wv_hi, k + 1)
                nc.gpsimd.tensor_tensor(wv[1][:, k, :], wv_nat[:, k, :], wv[0][:, k, :].bitcast(F32),
                                        ALU.subtract).then_inc(wv_split, 1)
            pool.wait_ge(adj_loaded, 16)
            nc.gpsimd.affine_select(out=mask[:, :, :], in_=mask[:, :, :], compare_op=ALU.not_equal, fill=0.0,
                                    base=0, pattern=[[P, T], [-1, N]], channel_multiplier=1).then_inc(mask_ready, 1)
            pool.wait_ge(neg_half_ready, 1)
            pool.wait_ge(mask_ready, 1)

            def inverse_norms(b):
                pool.wait_ge(r_clamped, b + 1)
                nc.gpsimd.tensor_tensor(r[:, :], nsq_max[:, :], neg_half[:, :], ALU.pow).then_inc(r_ready, 1)

            def scale_mask(stream, db, first=0):
                pool.wait_ge(evacuated, stream.upto(("r", db, 0)))
                for i in range(first, T):
                    nc.gpsimd.tensor_tensor(mask_r[:, i, :], mask[:, i, :], row[:, :], ALU.mult)\
                        .then_inc(mask_r_ready, 1)

            def inverse_deviations(b, row_tiles=range(T)):
                for i in row_tiles:
                    pool.wait_ge(var_ready, b * T + (i + 1))
                    nc.gpsimd.tensor_tensor(rstd[:, i:i + 1], var_eps[:, i:i + 1], neg_half[:, 0:1], ALU.pow)\
                        .then_inc(rstd_ready, 1)

            def batch(b, parity, stream):
                inverse_norms(b)
                scale_mask(stream, 0)
                inverse_deviations(b)

            def last_two(b, stream):
                inverse_norms(b)
                scale_mask(stream, 0)
                inverse_deviations(b, range(2))
                inverse_norms(b + 1)
                scale_mask(stream, 1, first=1)
                inverse_deviations(b, [2, 3])
                inverse_deviations(b + 1)

            all_batches(pool, batch, last_two)


_INS = ["x", "adj", "L0_gnn_W_lang", "L0_gnn_W_grav", "L0_gnn_W_V", "L0_gnn_W_O", "L0_gnn_gate_logit",
        "L0_gnn_log_sigma"]


def kernel(**inputs):
    import numpy as _np
    import concourse.bacc as _bacc
    from concourse import mybir as _mybir
    from concourse.bass_utils import run_bass_kernel_spmd as _run

    nc = _bacc.Bacc("TRN2", target_bir_lowering=False, num_devices=1)
    arrays, args = {}, []
    for name in _INS:
        a = _np.ascontiguousarray(inputs[name])
        if a.ndim < 2:
            a = a.reshape(1, 1)
        arrays[f"in_{name}_dram"] = a
        args.append(nc.dram_tensor(f"in_{name}_dram", a.shape, _mybir.dt.from_np(a.dtype), kind="ExternalInput").ap())
    shape = arrays["in_x_dram"].shape
    args.append(nc.dram_tensor("out_0_dram", shape, _mybir.dt.float32, kind="ExternalOutput").ap())
    graph_attention(nc, *args)
    r = _run(nc, [arrays], core_ids=[0])
    return r.results[0]["out_0_dram"]
```
